# Optimizing a Trainium2 kernel written in Bass

```python
import numpy as np
import jax
import jax.numpy as jnp

def _softmax(x, axis=-1):
    return jax.nn.softmax(x, axis=axis)

def _gelu(x):
    return jax.nn.gelu(x, approximate=True)

def _silu(x):
    return jax.nn.silu(x)

def _sigmoid(x):
    return jax.nn.sigmoid(x)

def _layernorm(x, axis=-1, eps=1e-05):
    m = jnp.mean(x, axis=axis, keepdims=True)
    v = jnp.var(x, axis=axis, keepdims=True)
    return (x - m) / jnp.sqrt(v + eps)

def _scatter_add(tgt, idx, src, axis=0):
    return tgt.at[idx].add(src)

def _segment_sum(src, seg, n):
    return jax.ops.segment_sum(src, seg, n)
kernel_name = 'mk_dlrm_tower_d1_rec_r8_de64e1'

def setup_inputs(seed: int=0):
    np.random.seed(seed)
    _w = jnp.asarray

    def _rec_inputs():
        import jax
        import jax.numpy as jnp
        _tk = jax.random.key(seed)
        dense_ctx = jax.random.normal(jax.random.fold_in(_tk, 190), (512, 16), jnp.float32)
        ids = jnp.stack([jax.random.randint(jax.random.fold_in(_tk, 200 + f), (512,), 0, v, jnp.int32) for f, v in enumerate([125000, 1250, 1250, 1000, 1250, 1250, 1000, 1250, 12500, 1250, 1250, 1000, 1000, 1250, 125000, 12500, 125000, 125000, 1000, 125000, 12500, 1000, 12500, 1000, 125000, 1250, 125000, 12500, 12500, 1000, 1250, 12500, 12500, 125000, 1250, 12500, 12500, 1250, 1000])], axis=1)
        tbl_0 = 0.05 * jax.random.normal(jax.random.fold_in(_tk, 500 + 0), (125000, 16), jnp.float32)
        tbl_1 = 0.05 * jax.random.normal(jax.random.fold_in(_tk, 500 + 1), (1250, 16), jnp.float32)
        tbl_2 = 0.05 * jax.random.normal(jax.random.fold_in(_tk, 500 + 2), (1250, 16), jnp.float32)
        tbl_3 = 0.05 * jax.random.normal(jax.random.fold_in(_tk, 500 + 3), (1000, 16), jnp.float32)
        tbl_4 = 0.05 * jax.random.normal(jax.random.fold_in(_tk, 500 + 4), (1250, 16), jnp.float32)
        tbl_5 = 0.05 * jax.random.normal(jax.random.fold_in(_tk, 500 + 5), (1250, 16), jnp.float32)
        tbl_6 = 0.05 * jax.random.normal(jax.random.fold_in(_tk, 500 + 6), (1000, 16), jnp.float32)
        tbl_7 = 0.05 * jax.random.normal(jax.random.fold_in(_tk, 500 + 7), (1250, 16), jnp.float32)
        tbl_8 = 0.05 * jax.random.normal(jax.random.fold_in(_tk, 500 + 8), (12500, 16), jnp.float32)
        tbl_9 = 0.05 * jax.random.normal(jax.random.fold_in(_tk, 500 + 9), (1250, 16), jnp.float32)
        tbl_10 = 0.05 * jax.random.normal(jax.random.fold_in(_tk, 500 + 10), (1250, 16), jnp.float32)
        tbl_11 = 0.05 * jax.random.normal(jax.random.fold_in(_tk, 500 + 11), (1000, 16), jnp.float32)
        tbl_12 = 0.05 * jax.random.normal(jax.random.fold_in(_tk, 500 + 12), (1000, 16), jnp.float32)
        tbl_13 = 0.05 * jax.random.normal(jax.random.fold_in(_tk, 500 + 13), (1250, 16), jnp.float32)
        tbl_14 = 0.05 * jax.random.normal(jax.random.fold_in(_tk, 500 + 14), (125000, 16), jnp.float32)
        tbl_15 = 0.05 * jax.random.normal(jax.random.fold_in(_tk, 500 + 15), (12500, 16), jnp.float32)
        tbl_16 = 0.05 * jax.random.normal(jax.random.fold_in(_tk, 500 + 16), (125000, 16), jnp.float32)
        tbl_17 = 0.05 * jax.random.normal(jax.random.fold_in(_tk, 500 + 17), (125000, 16), jnp.float32)
        tbl_18 = 0.05 * jax.random.normal(jax.random.fold_in(_tk, 500 + 18), (1000, 16), jnp.float32)
        tbl_19 = 0.05 * jax.random.normal(jax.random.fold_in(_tk, 500 + 19), (125000, 16), jnp.float32)
        tbl_20 = 0.05 * jax.random.normal(jax.random.fold_in(_tk, 500 + 20), (12500, 16), jnp.float32)
        tbl_21 = 0.05 * jax.random.normal(jax.random.fold_in(_tk, 500 + 21), (1000, 16), jnp.float32)
        tbl_22 = 0.05 * jax.random.normal(jax.random.fold_in(_tk, 500 + 22), (12500, 16), jnp.float32)
        tbl_23 = 0.05 * jax.random.normal(jax.random.fold_in(_tk, 500 + 23), (1000, 16), jnp.float32)
        tbl_24 = 0.05 * jax.random.normal(jax.random.fold_in(_tk, 500 + 24), (125000, 16), jnp.float32)
        tbl_25 = 0.05 * jax.random.normal(jax.random.fold_in(_tk, 500 + 25), (1250, 16), jnp.float32)
        tbl_26 = 0.05 * jax.random.normal(jax.random.fold_in(_tk, 500 + 26), (125000, 16), jnp.float32)
        tbl_27 = 0.05 * jax.random.normal(jax.random.fold_in(_tk, 500 + 27), (12500, 16), jnp.float32)
        tbl_28 = 0.05 * jax.random.normal(jax.random.fold_in(_tk, 500 + 28), (12500, 16), jnp.float32)
        tbl_29 = 0.05 * jax.random.normal(jax.random.fold_in(_tk, 500 + 29), (1000, 16), jnp.float32)
        tbl_30 = 0.05 * jax.random.normal(jax.random.fold_in(_tk, 500 + 30), (1250, 16), jnp.float32)
        tbl_31 = 0.05 * jax.random.normal(jax.random.fold_in(_tk, 500 + 31), (12500, 16), jnp.float32)
        tbl_32 = 0.05 * jax.random.normal(jax.random.fold_in(_tk, 500 + 32), (12500, 16), jnp.float32)
        tbl_33 = 0.05 * jax.random.normal(jax.random.fold_in(_tk, 500 + 33), (125000, 16), jnp.float32)
        tbl_34 = 0.05 * jax.random.normal(jax.random.fold_in(_tk, 500 + 34), (1250, 16), jnp.float32)
        tbl_35 = 0.05 * jax.random.normal(jax.random.fold_in(_tk, 500 + 35), (12500, 16), jnp.float32)
        tbl_36 = 0.05 * jax.random.normal(jax.random.fold_in(_tk, 500 + 36), (12500, 16), jnp.float32)
        tbl_37 = 0.05 * jax.random.normal(jax.random.fold_in(_tk, 500 + 37), (1250, 16), jnp.float32)
        tbl_38 = 0.05 * jax.random.normal(jax.random.fold_in(_tk, 500 + 38), (1000, 16), jnp.float32)
        _rk = jax.random.fold_in(_tk, 7)
        W_top1 = 0.05 * jax.random.normal(jax.random.fold_in(_tk, 801), (400, 512), jnp.float32)
        W_top2 = 0.0441942 * jax.random.normal(jax.random.fold_in(_tk, 802), (512, 256), jnp.float32)
        W_top3 = 0.0625 * jax.random.normal(jax.random.fold_in(_tk, 803), (256, 1), jnp.float32)
        b_top1 = jnp.zeros((512,), jnp.float32)
        b_top2 = jnp.zeros((256,), jnp.float32)
        return (dense_ctx, ids, tbl_0, tbl_1, tbl_2, tbl_3, tbl_4, tbl_5, tbl_6, tbl_7, tbl_8, tbl_9, tbl_10, tbl_11, tbl_12, tbl_13, tbl_14, tbl_15, tbl_16, tbl_17, tbl_18, tbl_19, tbl_20, tbl_21, tbl_22, tbl_23, tbl_24, tbl_25, tbl_26, tbl_27, tbl_28, tbl_29, tbl_30, tbl_31, tbl_32, tbl_33, tbl_34, tbl_35, tbl_36, tbl_37, tbl_38, W_top1, b_top1, W_top2, b_top2, W_top3)
    dense_ctx, ids, tbl_0, tbl_1, tbl_2, tbl_3, tbl_4, tbl_5, tbl_6, tbl_7, tbl_8, tbl_9, tbl_10, tbl_11, tbl_12, tbl_13, tbl_14, tbl_15, tbl_16, tbl_17, tbl_18, tbl_19, tbl_20, tbl_21, tbl_22, tbl_23, tbl_24, tbl_25, tbl_26, tbl_27, tbl_28, tbl_29, tbl_30, tbl_31, tbl_32, tbl_33, tbl_34, tbl_35, tbl_36, tbl_37, tbl_38, W_top1, b_top1, W_top2, b_top2, W_top3 = _rec_inputs()

    def _L0_rec_setup():
        import jax, jax.numpy as jnp
        import numpy as np
        B, F0, D = (256, 39, 16)
        CROSS = [128, 128, 128]
        key = jax.random.key(seed)
        k0, k1, k2, k3 = jax.random.split(key, 4)
        inputs = jax.random.normal(k0, (B, F0, D), dtype=jnp.float32)
        f0 = jax.random.normal(k1, (F0 * F0, CROSS[0]), dtype=jnp.float32) * 0.05
        f1 = jax.random.normal(k2, (CROSS[0] * F0, CROSS[1]), dtype=jnp.float32) * 0.05
        f2 = jax.random.normal(k3, (CROSS[1] * F0, CROSS[2]), dtype=jnp.float32) * 0.05
        return {'inputs': inputs, 'f0': f0, 'f1': f1, 'f2': f2}
    _L0_rec_all = _L0_rec_setup()
    _L0_rec_in = {k: v for k, v in _L0_rec_all.items() if k in ('f0', 'f1', 'f2')}
    del _L0_rec_all
    return {'dense_ctx': dense_ctx, 'ids': ids, 'tbl_0': tbl_0, 'tbl_1': tbl_1, 'tbl_2': tbl_2, 'tbl_3': tbl_3, 'tbl_4': tbl_4, 'tbl_5': tbl_5, 'tbl_6': tbl_6, 'tbl_7': tbl_7, 'tbl_8': tbl_8, 'tbl_9': tbl_9, 'tbl_10': tbl_10, 'tbl_11': tbl_11, 'tbl_12': tbl_12, 'tbl_13': tbl_13, 'tbl_14': tbl_14, 'tbl_15': tbl_15, 'tbl_16': tbl_16, 'tbl_17': tbl_17, 'tbl_18': tbl_18, 'tbl_19': tbl_19, 'tbl_20': tbl_20, 'tbl_21': tbl_21, 'tbl_22': tbl_22, 'tbl_23': tbl_23, 'tbl_24': tbl_24, 'tbl_25': tbl_25, 'tbl_26': tbl_26, 'tbl_27': tbl_27, 'tbl_28': tbl_28, 'tbl_29': tbl_29, 'tbl_30': tbl_30, 'tbl_31': tbl_31, 'tbl_32': tbl_32, 'tbl_33': tbl_33, 'tbl_34': tbl_34, 'tbl_35': tbl_35, 'tbl_36': tbl_36, 'tbl_37': tbl_37, 'tbl_38': tbl_38, 'W_top1': W_top1, 'b_top1': b_top1, 'W_top2': W_top2, 'b_top2': b_top2, 'W_top3': W_top3, 'L0_rec_f0': _L0_rec_in['f0'], 'L0_rec_f1': _L0_rec_in['f1'], 'L0_rec_f2': _L0_rec_in['f2']}

def reference(dense_ctx, ids, tbl_0, tbl_1, tbl_2, tbl_3, tbl_4, tbl_5, tbl_6, tbl_7, tbl_8, tbl_9, tbl_10, tbl_11, tbl_12, tbl_13, tbl_14, tbl_15, tbl_16, tbl_17, tbl_18, tbl_19, tbl_20, tbl_21, tbl_22, tbl_23, tbl_24, tbl_25, tbl_26, tbl_27, tbl_28, tbl_29, tbl_30, tbl_31, tbl_32, tbl_33, tbl_34, tbl_35, tbl_36, tbl_37, tbl_38, W_top1, b_top1, W_top2, b_top2, W_top3, L0_rec_f0, L0_rec_f1, L0_rec_f2):
    import jax
    import jax.numpy as jnp

    def _L0_rec_ref(inputs, f0, f1, f2):
        import jax, jax.numpy as jnp
        import numpy as np
        B, F0, D = (256, 39, 16)
        CROSS = [128, 128, 128]
        filters = [f0, f1, f2]
        x0 = inputs
        xk = inputs
        outs = []
        for W in filters:
            b, f, d = x0.shape
            g = xk.shape[1]
            z = jnp.einsum('bfd,bgd->bfgd', x0, xk).reshape(b, f * g, d)
            cur = jnp.einsum('bpd,pm->bmd', z, W)
            outs.append(cur)
            xk = cur
        result = jnp.concatenate(outs, axis=1)
        return jnp.sum(result, axis=-1)
    e = jnp.stack([tbl_0[ids[:, 0]], tbl_1[ids[:, 1]], tbl_2[ids[:, 2]], tbl_3[ids[:, 3]], tbl_4[ids[:, 4]], tbl_5[ids[:, 5]], tbl_6[ids[:, 6]], tbl_7[ids[:, 7]], tbl_8[ids[:, 8]], tbl_9[ids[:, 9]], tbl_10[ids[:, 10]], tbl_11[ids[:, 11]], tbl_12[ids[:, 12]], tbl_13[ids[:, 13]], tbl_14[ids[:, 14]], tbl_15[ids[:, 15]], tbl_16[ids[:, 16]], tbl_17[ids[:, 17]], tbl_18[ids[:, 18]], tbl_19[ids[:, 19]], tbl_20[ids[:, 20]], tbl_21[ids[:, 21]], tbl_22[ids[:, 22]], tbl_23[ids[:, 23]], tbl_24[ids[:, 24]], tbl_25[ids[:, 25]], tbl_26[ids[:, 26]], tbl_27[ids[:, 27]], tbl_28[ids[:, 28]], tbl_29[ids[:, 29]], tbl_30[ids[:, 30]], tbl_31[ids[:, 31]], tbl_32[ids[:, 32]], tbl_33[ids[:, 33]], tbl_34[ids[:, 34]], tbl_35[ids[:, 35]], tbl_36[ids[:, 36]], tbl_37[ids[:, 37]], tbl_38[ids[:, 38]]], axis=1)
    z = _L0_rec_ref(e, L0_rec_f0, L0_rec_f1, L0_rec_f2)
    z = z.reshape(z.shape[0], -1)
    h = jnp.concatenate([z, dense_ctx], axis=1)
    h = jnp.maximum(h @ W_top1 + b_top1, 0.0)
    h = jnp.maximum(h @ W_top2 + b_top2, 0.0)
    y = h @ W_top3
    return y

_drawn_inputs = setup_inputs


def setup_inputs(seed=0):
    import zlib

    import numpy as np

    out = dict(_drawn_inputs(seed))
    spreads = {'b_top1': (0.0, 0.613), 'b_top2': (0.0, 0.283)}
    factors = {'tbl_0': 4.765,
     'tbl_1': 4.903,
     'tbl_2': 4.496,
     'tbl_3': 4.794,
     'tbl_4': 4.988,
     'tbl_5': 4.911,
     'tbl_6': 4.6,
     'tbl_7': 4.852,
     'tbl_8': 5.236,
     'tbl_9': 4.488,
     'tbl_10': 5.269,
     'tbl_11': 4.776,
     'tbl_12': 4.494,
     'tbl_13': 4.474,
     'tbl_14': 4.574,
     'tbl_15': 4.706,
     'tbl_16': 5.181,
     'tbl_17': 4.683,
     'tbl_18': 5.015,
     'tbl_19': 4.791,
     'tbl_20': 4.872,
     'tbl_21': 4.899,
     'tbl_22': 4.822,
     'tbl_23': 4.729,
     'tbl_24': 4.702,
     'tbl_25': 4.448,
     'tbl_26': 4.964,
     'tbl_27': 5.022,
     'tbl_28': 4.622,
     'tbl_29': 4.382,
     'tbl_30': 4.942,
     'tbl_31': 4.407,
     'tbl_32': 4.793,
     'tbl_33': 4.623,
     'tbl_34': 4.855,
     'tbl_35': 4.643,
     'tbl_36': 4.867,
     'tbl_37': 4.99,
     'tbl_38': 5.136,
     'L0_rec_f1': 5.127,
     'L0_rec_f2': 8.0}
    for name, (base, spread) in spreads.items():
        noise = np.random.default_rng([zlib.crc32(name.encode()), seed]).standard_normal(out[name].shape)
        drawn = base * np.exp(spread * noise) if base else spread * noise
        out[name] = jnp.asarray(drawn.astype(out[name].dtype))
    for name, factor in factors.items():
        out[name] = (out[name] * factor).astype(out[name].dtype)
    return out
```

```python
from contextlib import ExitStack

import concourse.bass as bass
from concourse import mybir

B, F, D, M = 512, 39, 16, 128
FP = F + 1
ONE_ROW = F
LOW = 64
K0 = LOW + F
TILE = 128
TB = TILE // D
TPC = 4
CHUNK = TPC * TILE
CB = CHUNK // D
BATCH = 128
CPB = BATCH // CB
NB = B // BATCH
NCH = B // CB
NT = NCH * TPC
SHIFTS = F // 2 + 1
SPT = 3
ZT = -(-SHIFTS // SPT)
ZROWS = [F * min(SPT, SHIFTS - SPT * t) for t in range(ZT)]
ZMAX = max(ZROWS)
NZ = 4
FG = 4
GROUPS = [list(range(f, min(f + FG, F))) for f in range(0, F, FG)]
NG = len(GROUPS)
OWNER = "DADADADADD"
DF = sum(len(g) for g, o in zip(GROUPS, OWNER) if o == "D")
AG = OWNER.count("A")
NY = 4
DGROUPS = D // 4
H1, H2 = 512, 256
KD = 16
SELW = (ZT + 1) * ZMAX

STEPS = [["S0", "S1", "S2", "Z0", "S3"], ["Z1", "S4", "Z2", "S5", "Z3"], ["S6", "Z4", "S7", "Z5", "Z6"]]
PAIRS_AT = {(0, 4): 0, (0, 6): 1, (1, 0): 2, (1, 4): 3, (1, 8): 4, (2, 2): 5, (2, 6): 6}


def before(owner, g):
    mine = [GROUPS[i] for i in range(g) if OWNER[i] == owner]
    return len(mine), sum(len(x) for x in mine)


def tower_kernel(nc, args, out):
    fp32, f32r, i32 = mybir.dt.float32, mybir.dt.float32r, mybir.dt.int32
    ALU, ACT, AX = mybir.AluOpType, mybir.ActivationFunctionType, mybir.AxisListType
    tables = [args[f"tbl_{f}"] for f in range(F)]

    ctx = ExitStack()
    with ctx:
        def sb(name, shape, dt=fp32):
            return ctx.enter_context(nc.sbuf_tensor(name, shape, dt))

        def ps(name, cols=512):
            return ctx.enter_context(nc.psum_tensor(name, [128, cols], fp32))

        def sem(name):
            return ctx.enter_context(nc.semaphore(name))

        ident = sb("ident", [128, 128])
        mask = sb("mask", [128, TB])
        sel = sb("sel", [K0, SELW + FP], f32r)
        w0 = sb("w0", [ZMAX, ZT, M])
        w1h = sb("w1h", [128, F * M], f32r)
        w1l = sb("w1l", [128, F * M], f32r)
        w2 = sb("w2", [128, F, M])
        bias1 = sb("bias1", [128, H1 // 128])
        bias2 = sb("bias2", [128, H2 // 128])
        wt3 = sb("wt3", [128, H2 // 128])
        dense = sb("dense", [KD, B])
        ids_all = sb("ids_all", [128, NB, F], i32)
        ids_now = sb("ids_now", [128, F], i32)
        emb = sb("emb", [128, F, D])
        x0 = sb("x0", [K0, BATCH * D], f32r)
        x0c = sb("x0c", [K0, CHUNK], f32r)
        x0t = sb("x0t", [128, TPC, FP])
        spread = sb("spread", [ZMAX, CHUNK])
        pairs = sb("pairs", [128, NZ, CHUNK])
        x1h = sb("x1h", [128, CHUNK], f32r)
        x1l = sb("x1l", [128, CHUNK], f32r)
        accd = sb("accd", [128, 2, 2, M])
        prod = sb("prod", [128, 2, AG, FG * M])
        sum4 = sb("sum4", [128, FG * M])
        sum2 = sb("sum2", [128, 2 * M])
        sum1 = sb("sum1", [128, 3, M])
        x2 = sb("x2", [128, 2, M])
        diag = sb("diag", [128, 2, FP, TB])
        G = sb("G", [128, FP, B])
        out0 = sb("out0", [128, B])
        flat = G[:, :, :].rearrange("p f b -> p (f b)")
        w1raw = flat[:, 0:F * M]
        w0a = flat[0:ZMAX, F * M:F * M + ZT * M]
        w0b = flat[0:ZMAX, F * M + ZT * M:F * M + 2 * ZT * M]
        selraw = flat[0:K0, F * M + 2 * ZT * M:F * M + 2 * ZT * M + SELW + FP]
        h1 = [prod[:, 0, m, :] for m in range(H1 // 128)]
        wt1 = prod[:, 1, :, :]
        wt2 = pairs[:, 0:2, :].rearrange("p a (k n) -> p (a k) n", n=H2)
        h2 = [pairs[:, 2 + m, :] for m in range(H2 // 128)]
        out2 = sum4
        y = spread[0:1, :]

        Y = [ps(f"Y{i}") for i in range(NY)]
        S = [ps(f"S{i}") for i in range(2)]
        X1 = ps("X1")
        MISC = ps("MISC")
        XT = S[1][:, 0:TPC * FP].rearrange("p (k f) -> p k f", k=TPC)

        const_in = sem("const_in")
        ids_in = sem("ids_in")
        w1_in = [sem(f"w1_in{i}") for i in range(2)]
        w2_in = sem("w2_in")
        mlp_in = sem("mlp_in")
        sel_ready = sem("sel_ready")
        w0_ready = sem("w0_ready")
        w1h_ready = sem("w1h_ready")
        w1l_ready = sem("w1l_ready")
        ones_ready = sem("ones_ready")
        ids_ready = sem("ids_ready")
        emb_in = sem("emb_in")
        turned = sem("turned")
        x0h_ready = sem("x0h_ready")
        x0l_ready = sem("x0l_ready")
        x0c_ready = sem("x0c_ready")
        spread_done = sem("spread_done")
        spread_ready = sem("spread_ready")
        pairs_ready = sem("pairs_ready")
        pairs_used = sem("pairs_used")
        xt_done = sem("xt_done")
        xt_ready = sem("xt_ready")
        x1h_ready = sem("x1h_ready")
        x1l_ready = sem("x1l_ready")
        out0_ready = sem("out0_ready")
        y_done = sem("y_done")
        acc_step = sem("acc_step")
        prod_ready = sem("prod_ready")
        pool_step = sem("pool_step")
        diag_ready = sem("diag_ready")
        g_done = sem("g_done")
        g_stored = sem("g_stored")
        out2_done = sem("out2_done")
        out2_ready = sem("out2_ready")
        h1_done = sem("h1_done")
        h1_act = sem("h1_act")
        h1_dve = sem("h1_dve")
        h2_done = sem("h2_done")
        h2_act = sem("h2_act")
        h2_dve = sem("h2_dve")
        y_sum = sem("y_sum")
        y_ready = sem("y_ready")
        stored = sem("stored")

        POOL_STEPS = 7

        def x2_count(t):
            return POOL_STEPS * t + POOL_STEPS

        def chunks(eng, body):
            body(0, 1, 0, first=True)
            body(1, 2, 0)
            with eng.Fori(0, NB - 1) as i:
                body(i * CPB + 2, 3, i, turn=True)
                with eng.Fori(0, CPB - 1) as j:
                    body(i * CPB + 3 + j, j, i + 1)
            body(NCH - 2, 3, NB - 1)
            body(NCH - 1, 0, 0, last=True)

        block = ctx.enter_context(nc.Block())

        @block.sync
        def _(sp):
            sp.dma_start(ids_all[:, :, :], args["ids"].rearrange("(t p) f -> p t f", p=128)).then_inc(ids_in, 16)
            sp.dma_start(ident[:, :], args["c_ident"]).then_inc(const_in, 16)
            sp.dma_start(selraw, args["c_sel"]).then_inc(const_in, 16)
            sp.dma_start(mask[:, :], args["c_mask"]).then_inc(const_in, 16)
            sp.dma_start(w0a, args["w0a"]).then_inc(const_in, 16)
            sp.dma_start(w0b, args["w0b"]).then_inc(const_in, 16)
            half = 5 * FG * M
            sp.dma_start(w1raw[:, 0:half], args["w1"][:, 0:half]).then_inc(w1_in[0], 16)
            sp.dma_start(w1raw[:, half:F * M], args["w1"][:, half:F * M]).then_inc(w1_in[1], 16)
            sp.dma_start(w2[:, :, :].rearrange("p f m -> p (f m)"), args["w2"]).then_inc(w2_in, 16)
            sp.wait_ge(pool_step, POOL_STEPS * NT)
            w_top1 = args["W_top1"]
            sp.dma_start(wt1[:, 0:3, :], w_top1[0:3 * M, :].rearrange("(k p) n -> p k n", p=128)).then_inc(mlp_in, 16)
            sp.dma_start(wt1[0:KD, 3, :], w_top1[3 * M:3 * M + KD, :]).then_inc(mlp_in, 16)
            sp.dma_start(wt2[:, :, :], args["W_top2"].rearrange("(k p) n -> p k n", p=128)).then_inc(mlp_in, 16)
            sp.dma_start(bias1[:, :], args["b1"]).then_inc(mlp_in, 16)
            sp.dma_start(bias2[:, :], args["b2"]).then_inc(mlp_in, 16)
            sp.dma_start(wt3[:, :], args["w3"]).then_inc(mlp_in, 16)
            sp.dma_start(dense[:, :], args["dense"]).then_inc(mlp_in, 16)
            sp.wait_ge(y_ready, 1)
            sp.dma_start(out.rearrange("b o -> o b"), y).then_inc(stored, 16)
            sp.wait_ge(stored, 16)

        MLP_DMAS = 7

        @block.gpsimd
        def _(pool):
            def ids_of(batch):
                nc.gpsimd.tensor_copy(ids_now[:, :], ids_all[:, bass.ds(batch, 1), :].rearrange("p o f -> p (o f)")
                                      ).then_inc(ids_ready, 1)
                pool.wait_ge(ids_ready, batch + 1)

            def gather(f):
                nc.gpsimd.indirect_dma_start(
                    out=emb[:, f, :], out_offset=None, in_=tables[f],
                    in_offset=bass.IndirectOffsetOnAxis(ap=ids_now[:, f:f + 1], axis=0)).then_inc(emb_in, 16)

            def tile(c, k, first=False, gathers=()):
                t = c * TPC + k
                par = k % 2
                fresh = first and k < 2
                pool.wait_ge(xt_ready, c * 2 + (1 if k < TPC - 1 else 2))
                if not fresh:
                    pool.wait_ge(g_done, t - 1)
                nc.gpsimd.tensor_tensor(
                    diag[:, par, :, :], x0t[:, k, :].rearrange("p (f o) -> p f o", o=1).to_broadcast([128, FP, TB]),
                    mask[:, :].rearrange("p (o b) -> p o b", o=1).to_broadcast([128, FP, TB]),
                    ALU.mult).then_inc(diag_ready, 1)
                for f in gathers:
                    gather(f)
                pool.wait_ge(prod_ready, t * AG + 2)
                nc.gpsimd.tensor_tensor(sum4[:, :], prod[:, par, 0, :], prod[:, par, 1, :],
                                        ALU.add).then_inc(pool_step, 1)
                for a in range(2, AG):
                    pool.wait_ge(prod_ready, t * AG + a + 1)
                    pool.wait_ge(pool_step, t * POOL_STEPS + a - 1)
                    nc.gpsimd.tensor_tensor(sum4[:, :], sum4[:, :], prod[:, par, a, :],
                                            ALU.add).then_inc(pool_step, 1)
                pool.wait_ge(pool_step, t * POOL_STEPS + AG - 1)
                nc.gpsimd.tensor_tensor(sum2[:, :], sum4[:, 0:2 * M], sum4[:, 2 * M:4 * M],
                                        ALU.add).then_inc(pool_step, 1)
                pool.wait_ge(pool_step, t * POOL_STEPS + AG)
                nc.gpsimd.tensor_tensor(sum1[:, 0, :], sum2[:, 0:M], sum2[:, M:2 * M],
                                        ALU.add).then_inc(pool_step, 1)
                pool.wait_ge(acc_step, t * DF + DF)
                nc.gpsimd.tensor_tensor(sum1[:, 1, :], accd[:, par, 0, :], accd[:, par, 1, :],
                                        ALU.add).then_inc(pool_step, 1)
                pool.wait_ge(pool_step, t * POOL_STEPS + AG + 2)
                nc.gpsimd.tensor_tensor(x2[:, par, :], sum1[:, 0, :], sum1[:, 1, :], ALU.add).then_inc(pool_step, 1)

            nc.gpsimd.memset(x0[:, :].bitcast(fp32), 1.0).then_inc(ones_ready, 1)
            pool.wait_ge(ids_in, 16)
            ids_of(0)
            for f in range(F):
                gather(f)
            pool.wait_ge(emb_in, 16 * F)
            ids_of(1)
            pool.wait_ge(const_in, 16 * 5)
            pool.wait_ge(turned, DGROUPS)
            for t in range(2 * TPC):
                tile(t // TPC, t % TPC, first=t < TPC, gathers=range(t * F // (2 * TPC), (t + 1) * F // (2 * TPC)))
            n = (CPB - 1) * TPC
            with pool.Fori(0, NB - 2) as i:
                for k in range(TPC):
                    tile(i * CPB + 2, k)
                pool.wait_ge(emb_in, (i + 2) * (16 * F))
                ids_of(i + 2)
                pool.wait_ge(turned, (i + 2) * DGROUPS)
                for s in range(n):
                    tile(i * CPB + 3 + s // TPC, s % TPC, gathers=range(s * F // n, (s + 1) * F // n))
            with pool.Fori(NCH - 6, NCH) as c:
                for k in range(TPC):
                    tile(c, k)

        @block.scalar
        def _(act):
            def high_half(batch, q):
                act.wait_ge(turned, batch * DGROUPS + q + 1)
                nc.scalar.copy(x0[0:F, :].rearrange("p (b d) -> p d b", d=D)[:, 4 * q:4 * q + 4, :],
                               MISC[0:F, :].rearrange("p (d b) -> p d b", d=4)).then_inc(x0h_ready, 1)

            def take_chunk(c, j, batch, first=False):
                act.wait_ge(x0l_ready, batch * DGROUPS + DGROUPS)
                if not first:
                    act.wait_ge(xt_done, c)
                nc.scalar.copy(x0c[:, :], x0[:, bass.ds(j * CHUNK, CHUNK)].bitcast(fp32)).then_inc(x0c_ready, 1)

            def keep_spread(c, first=False):
                act.wait_ge(spread_done, c * (ZT + 1) + 1)
                if not first:
                    act.wait_ge(pairs_ready, c * ZT)
                nc.scalar.copy(spread[:, :], S[0][0:ZMAX, :]).then_inc(spread_ready, 1)

            def keep_xt(c, part):
                tiles = slice(0, TPC - 1) if part == 0 else slice(TPC - 1, TPC)
                act.wait_ge(xt_done, c + 1)
                nc.scalar.copy(x0t[:, tiles, :], XT[:, tiles, :]).then_inc(xt_ready, 1)

            def x1_high(c, part):
                cols = slice(0, CHUNK - TILE) if part == 0 else slice(CHUNK - TILE, CHUNK)
                act.wait_ge(pairs_used, c * ZT + ZT)
                if part == 1:
                    act.wait_ge(out0_ready, c + 1)
                nc.scalar.copy(x1h[:, cols], X1[:, cols]).then_inc(x1h_ready, 1)

            def store_g(t):
                act.wait_ge(g_done, t + 1)
                nc.scalar.copy(G[:, :, bass.ds(t * TB, TB)],
                               MISC[:, 0:FP * TB].rearrange("p (f b) -> p f b", f=FP)).then_inc(g_stored, 1)

            def body(c, j, batch, first=False, turn=False, last=False):
                for k in range(TPC):
                    t = c * TPC + k
                    par = k % 2
                    if k == 0 and not last:
                        take_chunk(c + 1, j, batch)
                    if k == 0 and not first:
                        act.wait_ge(y_done, c * (TPC * NG))
                        x1_high(c, 1)
                    if k == TPC - 1 and not last:
                        x1_high(c + 1, 0)
                    if not (first and k < 2):
                        store_g(t - 2)
                    for g in range(NG):
                        if OWNER[g] != "A":
                            continue
                        a = before("A", g)[0]
                        if g == 3 and k == 0 and not last:
                            keep_spread(c + 1)
                        if a == 0:
                            act.wait_ge(xt_ready, c * 2 + (1 if k < TPC - 1 else 2))
                            if not (first and k < 2):
                                act.wait_ge(pool_step, x2_count(t - 2))
                        act.wait_ge(y_done, t * NG + g + 1)
                        for i, f in enumerate(GROUPS[g]):
                            last_of = nc.scalar.activation(
                                prod[:, par, a, i * M:(i + 1) * M], Y[(k * NG + g) % NY][:, i * M:(i + 1) * M],
                                ACT.Copy, scale=x0t[:, k, f:f + 1])
                        last_of.then_inc(prod_ready, 1)
                        if g == 1 and k == 0 and not first:
                            act.wait_ge(acc_step, c * (TPC * DF))
                            act.wait_ge(diag_ready, c * TPC)
                            keep_xt(c, 1)
                        if g == 3 and k == TPC - 1 and not last:
                            act.wait_ge(acc_step, t * DF)
                            act.wait_ge(diag_ready, t)
                            keep_xt(c + 1, 0)
                        if g == 5 and turn:
                            act.wait_ge(x0c_ready, c + 2)
                            high_half(batch + 1, k)

            act.wait_ge(ones_ready, 1)
            for g in range(NG):
                act.wait_ge(w1_in[g // 5], 16)
                cols = slice(g * FG * M, min((g + 1) * FG, F) * M)
                nc.scalar.copy(w1h[:, cols], w1raw[:, cols]).then_inc(w1h_ready, 1)
            for q in range(DGROUPS):
                high_half(0, q)
            take_chunk(0, 0, 0, first=True)
            keep_spread(0, first=True)
            keep_xt(0, 0)
            keep_xt(0, 1)
            x1_high(0, 0)
            x1_high(0, 1)
            chunks(act, body)
            store_g(NT - 2)
            store_g(NT - 1)
            act.wait_ge(mlp_in, 16 * MLP_DMAS)
            for m in (1, 3):
                act.wait_ge(h1_done, m + 1)
                nc.scalar.activation(h1[m], Y[m][:, :], ACT.Relu, bias=bias1[:, m:m + 1]).then_inc(h1_act, 1)
            act.wait_ge(h2_done, 2)
            nc.scalar.activation(h2[1], S[1][:, :], ACT.Relu, bias=bias2[:, 1:2]).then_inc(h2_act, 1)

        @block.vector
        def _(dve):
            def low_half(batch, q):
                dve.wait_ge(x0h_ready, batch * DGROUPS + q + 1)
                nc.vector.tensor_tensor(
                    x0[LOW:K0, :].rearrange("p (b d) -> p d b", d=D)[:, 4 * q:4 * q + 4, :],
                    MISC[0:F, :].rearrange("p (d b) -> p d b", d=4),
                    x0[0:F, :].bitcast(fp32).rearrange("p (b d) -> p d b", d=D)[:, 4 * q:4 * q + 4, :],
                    ALU.subtract).then_inc(x0l_ready, 1)

            def form_pairs(c, z, first=False):
                rows = ZROWS[z]
                dve.wait_ge(spread_ready, c + 1)
                dve.wait_ge(spread_done, c * (ZT + 1) + z + 2)
                if not first or z >= NZ:
                    dve.wait_ge(pairs_used, c * ZT + (z - NZ + 1))
                nc.vector.tensor_tensor(pairs[0:rows, (z if z < NZ else z - NZ), :], S[(z + 1) % 2][0:rows, :],
                                        spread[0:rows, :], ALU.mult).then_inc(pairs_ready, 1)

            def x1_low(c, part):
                cols = slice(0, CHUNK - TILE) if part == 0 else slice(CHUNK - TILE, CHUNK)
                dve.wait_ge(x1h_ready, c * 2 + part + 1)
                nc.vector.tensor_tensor(x1l[:, cols], X1[:, cols], x1h[:, cols].bitcast(fp32),
                                        ALU.subtract).then_inc(x1l_ready, 1)

            def sum_out0(c):
                nc.vector.tensor_reduce(out0[:, bass.ds(c * CB, CB)], X1[:, :].rearrange("p (b d) -> p b d", d=D),
                                        AX.X, ALU.add).then_inc(out0_ready, 1)

            def body(c, j, batch, first=False, turn=False, last=False):
                for k in range(TPC):
                    t = c * TPC + k
                    par = k % 2
                    dve.wait_ge(xt_ready, c * 2 + (1 if k < TPC - 1 else 2))
                    if not (first and k < 2):
                        dve.wait_ge(pool_step, x2_count(t - 2))
                    for g in range(NG):
                        if OWNER[g] != "D":
                            continue
                        n = before("D", g)[1]
                        dve.wait_ge(y_done, t * NG + g + 1)
                        for i, f in enumerate(GROUPS[g]):
                            acc = accd[:, par, (n + i) % 2, :]
                            src = Y[(k * NG + g) % NY][:, i * M:(i + 1) * M]
                            if n + i < 2:
                                nc.vector.tensor_scalar(acc, src, x0t[:, k, f:f + 1], None,
                                                        ALU.mult).then_inc(acc_step, 1)
                            else:
                                dve.wait_ge(acc_step, t * DF + n + i - 1)
                                nc.vector.scalar_tensor_tensor(
                                    out=acc, in0=src, scalar=x0t[:, k, f:f + 1], in1=acc,
                                    op0=ALU.mult, op1=ALU.add).then_inc(acc_step, 1)
                        if (k, g) == (0, 0) and not first:
                            x1_low(c, 1)
                        if (k, g) in PAIRS_AT and not last:
                            form_pairs(c + 1, PAIRS_AT[k, g])
                        if (k, g) == (TPC - 1, 2) and not last:
                            x1_low(c + 1, 0)
                        if (k, g) == (TPC - 1, 6) and not last:
                            sum_out0(c + 1)
                        if g == 6 and turn:
                            low_half(batch + 1, k)

            dve.wait_ge(const_in, 16 * 5)
            nc.vector.tensor_copy(sel[:, :], selraw).then_inc(sel_ready, 1)
            nc.vector.tensor_tensor(w0[:, :, :].rearrange("p z m -> p (z m)"), w0a, w0b, ALU.add).then_inc(w0_ready, 1)
            for g in range(NG):
                dve.wait_ge(w1h_ready, g + 1)
                cols = slice(g * FG * M, min((g + 1) * FG, F) * M)
                nc.vector.tensor_tensor(w1l[:, cols], w1raw[:, cols], w1h[:, cols].bitcast(fp32),
                                        ALU.subtract).then_inc(w1l_ready, 1)
            dve.wait_ge(ones_ready, 1)
            for q in range(DGROUPS):
                low_half(0, q)
            for z in range(ZT):
                form_pairs(0, z, first=True)
            x1_low(0, 0)
            sum_out0(0)
            x1_low(0, 1)
            chunks(dve, body)
            dve.wait_ge(out2_done, 1)
            nc.vector.tensor_copy(out2[:, :], X1[:, :]).then_inc(out2_ready, 1)
            dve.wait_ge(mlp_in, 16 * MLP_DMAS)
            for m in (0, 2):
                dve.wait_ge(h1_done, m + 1)
                nc.vector.tensor_scalar(h1[m], Y[m][:, :], bias1[:, m:m + 1], 0.0, ALU.add,
                                        ALU.max).then_inc(h1_dve, 1)
            dve.wait_ge(h2_done, 1)
            nc.vector.tensor_scalar(h2[0], S[0][:, :], bias2[:, 0:1], 0.0, ALU.add, ALU.max).then_inc(h2_dve, 1)
            dve.wait_ge(y_sum, 1)
            nc.vector.tensor_copy(y, MISC[0:1, :]).then_inc(y_ready, 1)

        @block.tensor
        def _(pe):
            def await_components(batch, q):
                pe.wait_ge(emb_in, batch * (16 * F) + 16 * F)
                if q:
                    pe.wait_ge(x0l_ready, batch * DGROUPS + q)

            def turn_components(q):
                for i in range(4):
                    done = nc.tensor.transpose(MISC[0:F, i * 128:(i + 1) * 128], emb[:, :, 4 * q + i], ident[:, :])
                done.then_inc(turned, 1)

            def spread_x0(c, s, first=False):
                rows = ZMAX if s == 0 else ZROWS[s - 1]
                if s == 0:
                    pe.wait_ge(x0c_ready, c + 1)
                    if not first:
                        pe.wait_ge(pairs_ready, c * ZT)
                if s == 1:
                    pe.wait_ge(xt_ready, (c * 2 if not first else 2))
                if s == 2:
                    pe.wait_ge(spread_ready, c + 1)
                if s > 2:
                    pe.wait_ge(pairs_ready, c * ZT + s - 2)
                nc.tensor.matmul(S[s % 2][0:rows, :], sel[:, s * ZMAX:s * ZMAX + rows], x0c[:, :],
                                 start=True, stop=True).then_inc(spread_done, 1)

            def weigh_pairs(c, z, first=False):
                pe.wait_ge(pairs_ready, c * ZT + z + 1)
                if z == 0 and not first:
                    pe.wait_ge(x1l_ready, c * 2)
                    pe.wait_ge(out0_ready, c)
                rows = ZROWS[z]
                nc.tensor.matmul(X1[:, :], w0[0:rows, z, :], pairs[0:rows, z % NZ, :],
                                 start=(z == 0), stop=(z == ZT - 1)).then_inc(pairs_used, 1)

            def turn_x0(c, first=False):
                if not first:
                    pe.wait_ge(pairs_ready, c * ZT + ZT)
                for k in range(TPC):
                    done = nc.tensor.matmul(XT[:, k, :], x0c[:, k * TILE:(k + 1) * TILE],
                                            sel[:, SELW:SELW + FP], start=True, stop=True)
                done.then_inc(xt_done, 1)

            def g_part(t, par, after_turn=None, first=False):
                pe.wait_ge(pool_step, x2_count(t))
                pe.wait_ge(diag_ready, t + 1)
                if not first:
                    pe.wait_ge(g_stored, t)
                if after_turn is not None:
                    pe.wait_ge(x0l_ready, after_turn)
                nc.tensor.matmul(MISC[:, 0:FP * TB], x2[:, par, :], diag[:, par, :, :].rearrange("p f b -> p (f b)"),
                                 start=True, stop=True).then_inc(g_done, 1)

            def step(c, what):
                if what[0] == "S":
                    spread_x0(c, int(what[1]))
                else:
                    weigh_pairs(c, int(what[1]))

            def bank_free(c, k, g, first):
                q = k * NG + g - NY
                if q < 0 and first:
                    return
                t = c * TPC + (q // NG)
                gg = q % NG
                if OWNER[gg] == "D":
                    pe.wait_ge(acc_step, t * DF + (before("D", gg)[1] + len(GROUPS[gg])))
                else:
                    pe.wait_ge(prod_ready, t * AG + (before("A", gg)[0] + 1))

            def body(c, j, batch, first=False, turn=False, last=False):
                for k in range(TPC):
                    if k == 0:
                        pe.wait_ge(x1l_ready, c * 2 + 1)
                    if k == TPC - 1:
                        pe.wait_ge(x1l_ready, c * 2 + 2)
                    for g in range(NG):
                        if first and k == 0:
                            pe.wait_ge(w1l_ready, g + 1)
                        if g == 4 and turn:
                            await_components(batch + 1, k)
                            pe.wait_ge(g_stored, c * TPC + k - 1)
                        bank_free(c, k, g, first)
                        cols = slice(g * FG * M, min((g + 1) * FG, F) * M)
                        out_y = Y[(k * NG + g) % NY][:, 0:cols.stop - cols.start]
                        here = slice(k * TILE, (k + 1) * TILE)
                        nc.tensor.matmul(out_y, x1h[:, here], w1h[:, cols], start=True, stop=False)
                        nc.tensor.matmul(out_y, x1h[:, here], w1l[:, cols], start=False, stop=False)
                        nc.tensor.matmul(out_y, x1l[:, here], w1h[:, cols], start=False,
                                         stop=True).then_inc(y_done, 1)
                        if g == 1 and k == TPC - 1 and not last:
                            turn_x0(c + 1)
                        if g % 2 == 1 and k < TPC - 1 and not last:
                            step(c + 1, STEPS[k][g // 2])
                        if g == 4 and turn:
                            turn_components(k)
                        if g == 8 and not (first and k == 0):
                            g_part(c * TPC + k - 1, (k + 1) % 2, first=first and k == 1,
                                   after_turn=batch * DGROUPS + DGROUPS + k + 1 if turn else None)

            pe.wait_ge(const_in, 16 * 5)
            for q in range(DGROUPS):
                await_components(0, q)
                turn_components(q)
            pe.wait_ge(sel_ready, 1)
            pe.wait_ge(x0c_ready, 1)
            turn_x0(0, first=True)
            spread_x0(0, 0, first=True)
            spread_x0(0, 1, first=True)
            pe.wait_ge(w0_ready, 1)
            for z in range(ZT):
                if z + 2 <= ZT:
                    spread_x0(0, z + 2, first=True)
                weigh_pairs(0, z, first=True)
            chunks(pe, body)
            g_part(NT - 1, (NT - 1) % 2)
            pe.wait_ge(w2_in, 16)
            pe.wait_ge(g_stored, NT)
            for f in range(F):
                done = nc.tensor.matmul(X1[:, :], w2[:, f, :], G[:, f, :], start=(f == 0), stop=(f == F - 1))
            done.then_inc(out2_done, 1)
            pe.wait_ge(mlp_in, 16 * MLP_DMAS)
            for part, (rows, src) in enumerate([(M, out0[:, :]), (M, G[:, F, :]), (KD, dense[:, :]),
                                                (M, out2[:, :])]):
                if part == 3:
                    pe.wait_ge(out2_ready, 1)
                kt = [0, 1, 3, 2][part]
                for m in range(H1 // 128):
                    done = nc.tensor.matmul(Y[m][:, :], wt1[0:rows, kt, m * 128:(m + 1) * 128], src,
                                            start=(part == 0), stop=(part == 3))
                    if part == 3:
                        done.then_inc(h1_done, 1)
            for m in range(H2 // 128):
                for kt in range(H1 // 128):
                    if m == 0:
                        if kt % 2:
                            pe.wait_ge(h1_act, kt // 2 + 1)
                        else:
                            pe.wait_ge(h1_dve, kt // 2 + 1)
                    done = nc.tensor.matmul(S[m][:, :], wt2[:, kt, m * 128:(m + 1) * 128], h1[kt],
                                            start=(kt == 0), stop=(kt == H1 // 128 - 1))
                done.then_inc(h2_done, 1)
            pe.wait_ge(h2_dve, 1)
            nc.tensor.matmul(MISC[0:1, :], wt3[:, 0:1], h2[0], start=True, stop=False)
            pe.wait_ge(h2_act, 1)
            nc.tensor.matmul(MISC[0:1, :], wt3[:, 1:2], h2[1], start=False, stop=True).then_inc(y_sum, 1)


def constants(np):
    sel = np.zeros((K0, SELW + FP), np.float32)
    for s in range(ZT + 1):
        for j in range(SPT):
            shift = 0 if s == 0 else SPT * (s - 1) + j
            if shift < SHIFTS:
                for f in range(F):
                    sel[(f + shift) % F, s * ZMAX + j * F + f] = 1.0
                    sel[LOW + (f + shift) % F, s * ZMAX + j * F + f] = 1.0
    for f in range(F):
        sel[f, SELW + f] = sel[LOW + f, SELW + f] = 1.0
    sel[ONE_ROW, SELW + F] = 1.0
    mask = np.zeros((128, TB), np.float32)
    mask[np.arange(128), np.arange(128) // D] = 1.0
    return {"c_sel": sel, "c_mask": mask, "c_ident": np.eye(128, dtype=np.float32)}


def kernel(**inputs):
    import numpy as _np
    import concourse.bacc as _bacc
    from concourse import mybir as _mybir
    from concourse.bass_utils import run_bass_kernel_spmd as _run

    a = {k: _np.asarray(v) for k, v in inputs.items()}
    w0 = a["L0_rec_f0"].reshape(F, F, M)
    w0a = _np.zeros((ZMAX, ZT, M), _np.float32)
    w0b = _np.zeros((ZMAX, ZT, M), _np.float32)
    for s in range(SHIFTS):
        f = _np.arange(F)
        rows = (s % SPT) * F + f
        w0a[rows, s // SPT] = w0[f, (f + s) % F]
        if s:
            w0b[rows, s // SPT] = w0[(f + s) % F, f]
    arrays = {f"tbl_{f}": a[f"tbl_{f}"] for f in range(F)}
    arrays.update(constants(_np))
    arrays.update({
        "ids": a["ids"], "w0a": w0a.reshape(ZMAX, ZT * M), "w0b": w0b.reshape(ZMAX, ZT * M),
        "w1": a["L0_rec_f1"].reshape(F, M, M).transpose(1, 0, 2).reshape(M, F * M),
        "w2": a["L0_rec_f2"].reshape(F, M, M).transpose(1, 0, 2).reshape(M, F * M),
        "W_top1": a["W_top1"], "W_top2": a["W_top2"],
        "b1": a["b_top1"].reshape(H1 // 128, 128).T, "b2": a["b_top2"].reshape(H2 // 128, 128).T,
        "w3": a["W_top3"].reshape(H2 // 128, 128).T, "dense": a["dense_ctx"].T,
    })
    nc = _bacc.Bacc("TRN2", target_bir_lowering=False, num_devices=1)
    placed, args = {}, {}
    for name, v in arrays.items():
        v = _np.ascontiguousarray(v)
        placed[f"in_{name}"] = v
        args[name] = nc.dram_tensor(f"in_{name}", v.shape, _mybir.dt.from_np(v.dtype), kind="ExternalInput").ap()
    out = nc.dram_tensor("out_y", (B, 1), _mybir.dt.float32, kind="ExternalOutput").ap()
    tower_kernel(nc, args, out)
    r = _run(nc, [placed], core_ids=[0])
    return r.results[0]["out_y"]
```

```python
from contextlib import ExitStack

import concourse.bass as bass
from concourse import mybir

B, F, D, M = 512, 39, 16, 128
FP = F + 1
TILE = 128
TB = TILE // D
TPC = 4
CHUNK = TPC * TILE
CB = CHUNK // D
GS = 3
GPC = -(-CB // GS)
EARLY = 6
GATHERS_AT = [range(6, 9), range(9, GPC), range(0, 3), range(3, 6)]
GROWS = GS * F
FULL = CB - (GS - 1) * GPC
NCH = B // CB
NT = NCH * TPC
SHIFTS = F // 2 + 1
SPT = 3
ZT = -(-SHIFTS // SPT)
ZROWS = [F * min(SPT, SHIFTS - SPT * t) for t in range(ZT)]
ZMAX = max(ZROWS)
NZ = 4
FG = 4
GROUPS = [list(range(f, min(f + FG, F))) for f in range(0, F, FG)]
NG = len(GROUPS)
OWNER = "DADDADDADD"
DF = sum(len(g) for g, o in zip(GROUPS, OWNER) if o == "D")
AG = OWNER.count("A")
A_WIDTH = [len(g) * M for g, o in zip(GROUPS, OWNER) if o == "A"]
NY = 5
H1, H2 = 512, 256
KD = 16
LOADS = ZT + 1

PAIRS_AT = {(0, 0): 0, (0, 3): 1, (0, 6): 2, (0, 9): 3, (1, 3): 4, (1, 6): 5, (1, 9): 6}
WEIGH_AT = {(0, 6): 0, (0, 9): 1, (1, 2): 2, (1, 5): 3, (1, 9): 4, (2, 2): 5, (2, 5): 6}
TURN_AT = (2, 1)


def before(owner, g):
    mine = [GROUPS[i] for i in range(g) if OWNER[i] == owner]
    return len(mine), sum(len(x) for x in mine)


def tower_kernel(nc, args, out):
    fp32, f32r, i32 = mybir.dt.float32, mybir.dt.float32r, mybir.dt.int32
    ALU, ACT, AX = mybir.AluOpType, mybir.ActivationFunctionType, mybir.AxisListType
    ctx = ExitStack()
    with ctx:
        def sb(name, shape, dt=fp32):
            return ctx.enter_context(nc.sbuf_tensor(name, shape, dt))

        def ps(name, cols=512):
            return ctx.enter_context(nc.psum_tensor(name, [128, cols], fp32))

        def sem(name):
            return ctx.enter_context(nc.semaphore(name))

        ident = sb("ident", [128, 128])
        mask = sb("mask", [128, TB])
        base = sb("base", [GROWS, 1], i32)
        w0 = sb("w0", [ZMAX, ZT, M])
        w1h = sb("w1h", [128, F * M], f32r)
        w1l = sb("w1l", [128, F * M], f32r)
        w2 = sb("w2", [128, F, M])
        bias1 = sb("bias1", [128, H1 // 128])
        bias2 = sb("bias2", [128, H2 // 128])
        wt3 = sb("wt3", [128, H2 // 128])
        dense = sb("dense", [KD, B])
        ids_all = sb("ids_all", [GROWS, NCH, GPC], i32)
        rows_all = sb("rows_all", [GROWS, NCH, GPC], i32)
        rows_now = sb("rows_now", [GROWS, GPC], i32)
        emb = sb("emb", [GROWS, GPC, D])
        x0t = sb("x0t", [128, TPC, F])
        spread = sb("spread", [ZMAX, CHUNK])
        rot = sb("rot", [128, ZT, CHUNK])
        pairs = sb("pairs", [128, NZ, CHUNK])
        x1h = sb("x1h", [128, CHUNK], f32r)
        x1l = sb("x1l", [128, CHUNK], f32r)
        accd = sb("accd", [128, 2, 2, M])
        prod = sb("prod", [128, 2, AG, FG * M])
        sum4 = sb("sum4", [128, FG * M])
        sum2 = sb("sum2", [128, 2 * M])
        sum1 = sb("sum1", [128, 3, M])
        x2 = sb("x2", [128, 2, M])
        diag = sb("diag", [128, TPC, TB, FP])
        G = sb("G", [128, FP, B])
        out0 = sb("out0", [128, B])
        flat = G[:, :, :].rearrange("p f b -> p (f b)")
        w1raw = flat[:, 0:F * M]
        w0a = flat[0:ZMAX, F * M:F * M + ZT * M]
        w0b = flat[0:ZMAX, F * M + ZT * M:F * M + 2 * ZT * M]
        h1 = [rot[:, m, :] for m in range(H1 // 128)]
        wt1 = prod[:, :, :, :].rearrange("p a g n -> p (a g n)")[:, 0:4 * H1].rearrange("p (k n) -> p k n", k=4)
        wt2 = pairs[:, 0:2, :].rearrange("p a (k n) -> p (a k) n", n=H2)
        h2 = [pairs[:, 2 + m, :] for m in range(H2 // 128)]
        out2 = sum4
        y = spread[0:1, :]

        Y = [ps(f"Y{i}") for i in range(NY)]
        X1 = ps("X1")
        MISC = ps("MISC")
        XTB = ps("XTB")
        XT = XTB[:, 0:TPC * F].rearrange("p (k f) -> p k f", k=TPC)
        H2P = [Y[4], XTB]

        scratch_t = nc.dram_tensor("x0_scratch", (2 * F, CHUNK), fp32)
        scratch = scratch_t.ap()

        ids_in = sem("ids_in")
        const_in = sem("const_in")
        w0_in = sem("w0_in")
        w1_in = [sem(f"w1_in{i}") for i in range(2)]
        w2_in = sem("w2_in")
        mlp_in = sem("mlp_in")
        rows_ready = sem("rows_ready")
        rows_set = sem("rows_set")
        emb_in = sem("emb_in")
        scratch_in = sem("scratch_in")
        rot_in = sem("rot_in")
        w0_ready = sem("w0_ready")
        w1h_ready = sem("w1h_ready")
        w1l_ready = sem("w1l_ready")
        diag_clear = sem("diag_clear")
        pairs_ready = sem("pairs_ready")
        pairs_used = sem("pairs_used")
        xt_done = sem("xt_done")
        xt_ready = sem("xt_ready")
        diag_ready = sem("diag_ready")
        x1h_ready = sem("x1h_ready")
        x1l_ready = sem("x1l_ready")
        out0_ready = sem("out0_ready")
        y_done = sem("y_done")
        acc_step = sem("acc_step")
        prod_ready = sem("prod_ready")
        pool_step = sem("pool_step")
        g_done = sem("g_done")
        g_stored = sem("g_stored")
        out2_done = sem("out2_done")
        out2_ready = sem("out2_ready")
        h1_done = sem("h1_done")
        h1_act = sem("h1_act")
        h1_dve = sem("h1_dve")
        h2_done = sem("h2_done")
        h2_act = sem("h2_act")
        h2_dve = sem("h2_dve")
        y_sum = sem("y_sum")
        y_ready = sem("y_ready")
        stored = sem("stored")

        POOL_STEPS = AG + 3
        CONST_DMAS, MLP_DMAS = 2, 7

        def x2_count(t):
            return POOL_STEPS * t + POOL_STEPS

        def chunks(eng, body):
            body(0, first=True)
            with eng.Fori(1, NCH - 1) as c:
                body(c)
            body(NCH - 1, last=True)

        def group_cols(g):
            return slice(g * FG * M, min((g + 1) * FG, F) * M)

        block = ctx.enter_context(nc.Block())

        @block.sync
        def _(sp):
            def store_x0(c, before=None):
                sp.wait_ge(emb_in, c * (16 * GPC) + 16 * GPC)
                if before is not None:
                    sp.wait_ge(rot_in, before * (16 * LOADS) + 16 * LOADS)
                for s in range(GS):
                    n = GPC if s < GS - 1 else FULL
                    src = emb[s * F:(s + 1) * F, 0:n, :].rearrange("f i d -> f (i d)")
                    for copy in range(2):
                        sp.dma_start(scratch[copy * F:(copy + 1) * F, s * GPC * D:(s * GPC + n) * D],
                                     src).then_inc(scratch_in, 16)

            def load_x0(c, before=None):
                sp.wait_ge(scratch_in, c * (16 * 2 * GS) + 16 * 2 * GS)
                if before is not None:
                    sp.wait_ge(pairs_ready, before * ZT + ZT)
                for z in range(ZT):
                    sp.dma_start(rot[0:ZROWS[z], z, :],
                                 bass.AP(tensor=scratch_t, offset=SPT * z * CHUNK,
                                         ap=[[CHUNK, ZROWS[z] // F], [CHUNK, F], [1, CHUNK]])).then_inc(rot_in, 16)
                if before is not None:
                    sp.wait_ge(xt_done, c)
                sp.dma_start(spread[:, :], bass.AP(tensor=scratch_t, offset=0, ap=[[0, SPT], [CHUNK, F], [1, CHUNK]])
                             ).then_inc(rot_in, 16)

            sp.dma_start(ids_all[:, :, :].rearrange("p c i -> p (c i)"), args["ids"]).then_inc(ids_in, 16)
            sp.dma_start(base[:, :], args["base"]).then_inc(ids_in, 16)
            sp.dma_start(ident[:, :], args["c_ident"]).then_inc(const_in, 16)
            sp.dma_start(mask[:, :], args["c_mask"]).then_inc(const_in, 16)
            sp.dma_start(w0a, args["w0a"]).then_inc(w0_in, 16)
            sp.dma_start(w0b, args["w0b"]).then_inc(w0_in, 16)
            half = 5 * FG * M
            sp.dma_start(w1raw[:, 0:half], args["w1"][:, 0:half]).then_inc(w1_in[0], 16)
            sp.dma_start(w1raw[:, half:F * M], args["w1"][:, half:F * M]).then_inc(w1_in[1], 16)
            store_x0(0)
            load_x0(0)
            sp.dma_start(w2[:, :, :].rearrange("p f m -> p (f m)"), args["w2"]).then_inc(w2_in, 16)
            with sp.Fori(0, NCH - 1) as c:
                store_x0(c + 1, before=c)
                load_x0(c + 1, before=c)
            sp.dma_start(bias1[:, :], args["b1"]).then_inc(mlp_in, 16)
            sp.dma_start(bias2[:, :], args["b2"]).then_inc(mlp_in, 16)
            sp.dma_start(wt3[:, :], args["w3"]).then_inc(mlp_in, 16)
            sp.dma_start(dense[:, :], args["dense"]).then_inc(mlp_in, 16)
            sp.wait_ge(pool_step, POOL_STEPS * NT)
            w_top1 = args["W_top1"]
            sp.dma_start(wt1[:, 0:3, :], w_top1[0:3 * M, :].rearrange("(k p) n -> p k n", p=128)).then_inc(mlp_in, 16)
            sp.dma_start(wt1[0:KD, 3, :], w_top1[3 * M:3 * M + KD, :]).then_inc(mlp_in, 16)
            sp.dma_start(wt2, args["W_top2"].rearrange("(k p) n -> p k n", p=128)).then_inc(mlp_in, 16)
            sp.wait_ge(y_ready, 1)
            sp.dma_start(out.rearrange("b o -> o b"), y).then_inc(stored, 16)
            sp.wait_ge(stored, 16)

        @block.gpsimd
        def _(pool):
            def set_rows(c, first=False):
                if not first:
                    pool.wait_ge(emb_in, c * (16 * GPC))
                    pool.wait_ge(scratch_in, c * (16 * 2 * GS))
                nc.gpsimd.tensor_copy(rows_now[:, :], rows_all[:, bass.ds(c, 1), :].rearrange("p o i -> p (o i)")
                                      ).then_inc(rows_set, 1)

            def gather(i):
                n = GROWS if i < FULL else GROWS - F
                nc.gpsimd.indirect_dma_start(
                    out=emb[0:n, i, :], out_offset=None, in_=args["tables"],
                    in_offset=bass.IndirectOffsetOnAxis(ap=rows_now[0:n, i:i + 1], axis=0)).then_inc(emb_in, 16)

            def body(c, first=False, gathers=(True, True)):
                for k in range(TPC):
                    t = c * TPC + k
                    par = k % 2
                    fresh = first and k < 2
                    if k == 2 and gathers[1]:
                        set_rows(c + 3)
                        pool.wait_ge(rows_set, c + 4)
                    pool.wait_ge(prod_ready, t * AG + 2)
                    nc.gpsimd.tensor_tensor(sum4[:, :], prod[:, par, 0, :], prod[:, par, 1, :],
                                            ALU.add).then_inc(pool_step, 1)
                    if gathers[k // 2]:
                        for i in GATHERS_AT[k]:
                            gather(i)
                    for a in range(2, AG):
                        n = A_WIDTH[a]
                        pool.wait_ge(prod_ready, t * AG + a + 1)
                        pool.wait_ge(pool_step, t * POOL_STEPS + a - 1)
                        nc.gpsimd.tensor_tensor(sum4[:, 0:n], sum4[:, 0:n], prod[:, par, a, 0:n],
                                                ALU.add).then_inc(pool_step, 1)
                    pool.wait_ge(pool_step, t * POOL_STEPS + AG - 1)
                    nc.gpsimd.tensor_tensor(sum2[:, :], sum4[:, 0:2 * M], sum4[:, 2 * M:4 * M],
                                            ALU.add).then_inc(pool_step, 1)
                    pool.wait_ge(pool_step, t * POOL_STEPS + AG)
                    nc.gpsimd.tensor_tensor(sum1[:, 0, :], sum2[:, 0:M], sum2[:, M:2 * M],
                                            ALU.add).then_inc(pool_step, 1)
                    pool.wait_ge(acc_step, t * DF + DF)
                    nc.gpsimd.tensor_tensor(sum1[:, 1, :], accd[:, par, 0, :], accd[:, par, 1, :],
                                            ALU.add).then_inc(pool_step, 1)
                    pool.wait_ge(pool_step, t * POOL_STEPS + AG + 2)
                    if not fresh:
                        pool.wait_ge(g_done, t - 1)
                    nc.gpsimd.tensor_tensor(x2[:, par, :], sum1[:, 0, :], sum1[:, 1, :],
                                            ALU.add).then_inc(pool_step, 1)

            pool.wait_ge(ids_in, 32)
            nc.gpsimd.tensor_tensor(rows_all[:, :, :].rearrange("p c i -> p (c i)"),
                                    ids_all[:, :, :].rearrange("p c i -> p (c i)"),
                                    base[:, :].to_broadcast([GROWS, NCH * GPC]), ALU.add).then_inc(rows_ready, 1)
            pool.wait_ge(rows_ready, 1)
            for c in range(3):
                set_rows(c, first=c == 0)
                pool.wait_ge(rows_set, c + 1)
                for i in range(GPC if c < 2 else EARLY):
                    gather(i)
            body(0, first=True)
            with pool.Fori(1, NCH - 3) as c:
                body(c)
            body(NCH - 3, gathers=(True, False))
            with pool.Fori(NCH - 2, NCH) as c:
                body(c, gathers=(False, False))

        @block.scalar
        def _(act):
            def keep_xt(c, part):
                tiles = slice(0, TPC - 1) if part == 0 else slice(TPC - 1, TPC)
                act.wait_ge(xt_done, c + 1)
                nc.scalar.copy(x0t[:, tiles, :], XT[:, tiles, :]).then_inc(xt_ready, 1)

            def fill_diag(half):
                for b in range(half * TB // 2, (half + 1) * TB // 2):
                    rows = slice(b * D // 32 * 32, b * D // 32 * 32 + 32)
                    done = nc.scalar.activation(diag[rows, :, b, 0:F], XT[rows, :, :], ACT.Copy,
                                                scale=mask[rows, b:b + 1])
                if half:
                    done.then_inc(diag_ready, 1)

            def x1_high(c, part):
                cols = slice(0, CHUNK - TILE) if part == 0 else slice(CHUNK - TILE, CHUNK)
                act.wait_ge(pairs_used, c * ZT + ZT)
                if part == 1:
                    act.wait_ge(out0_ready, c + 1)
                nc.scalar.copy(x1h[:, cols], X1[:, cols]).then_inc(x1h_ready, 1)

            def store_g(t):
                act.wait_ge(g_done, t + 1)
                nc.scalar.copy(G[:, :, bass.ds(t * TB, TB)].rearrange("p f b -> p b f"),
                               MISC[:, 0:FP * TB].rearrange("p (b f) -> p b f", f=FP)).then_inc(g_stored, 1)

            def body(c, first=False, last=False):
                for k in range(TPC):
                    t = c * TPC + k
                    par = k % 2
                    if k == 0 and not first:
                        act.wait_ge(y_done, t * NG)
                        x1_high(c, 1)
                    if k == TPC - 1 and not last:
                        act.wait_ge(y_done, t * NG)
                        x1_high(c + 1, 0)
                    if not (first and k < 2):
                        store_g(t - 2)
                    for g in range(NG):
                        if OWNER[g] != "A":
                            continue
                        a = before("A", g)[0]
                        if a == 0:
                            act.wait_ge(xt_ready, c * 2 + (1 if k < TPC - 1 else 2))
                            if not (first and k < 2):
                                act.wait_ge(pool_step, x2_count(t - 2))
                        act.wait_ge(y_done, t * NG + g + 1)
                        for i, f in enumerate(GROUPS[g]):
                            done = nc.scalar.activation(
                                prod[:, par, a, i * M:(i + 1) * M], Y[(k * NG + g) % NY][:, i * M:(i + 1) * M],
                                ACT.Copy, scale=x0t[:, k, f:f + 1])
                        done.then_inc(prod_ready, 1)
                        if a == 0 and k == 0 and not first:
                            act.wait_ge(acc_step, t * DF)
                            act.wait_ge(prod_ready, t * AG)
                            keep_xt(c, 1)
                        if a < 2 and k == 1 and not first:
                            fill_diag(a)
                        if a == 1 and k == TPC - 1 and not last:
                            act.wait_ge(acc_step, t * DF)
                            act.wait_ge(prod_ready, t * AG)
                            keep_xt(c + 1, 0)

            for g in range(NG):
                act.wait_ge(w1_in[g // 5], 16)
                nc.scalar.copy(w1h[:, group_cols(g)], w1raw[:, group_cols(g)]).then_inc(w1h_ready, 1)
            keep_xt(0, 0)
            keep_xt(0, 1)
            act.wait_ge(diag_clear, 2)
            fill_diag(0)
            fill_diag(1)
            x1_high(0, 0)
            x1_high(0, 1)
            chunks(act, body)
            store_g(NT - 2)
            store_g(NT - 1)
            act.wait_ge(mlp_in, 16 * MLP_DMAS)
            for m in range(1, H1 // 128, 2):
                act.wait_ge(h1_done, m + 1)
                nc.scalar.activation(h1[m], Y[m][:, :], ACT.Relu, bias=bias1[:, m:m + 1]).then_inc(h1_act, 1)
            act.wait_ge(h2_done, 2)
            nc.scalar.activation(h2[1], H2P[1][:, :], ACT.Relu, bias=bias2[:, 1:2]).then_inc(h2_act, 1)

        @block.vector
        def _(dve):
            def form_pairs(c, z, first=False):
                rows = ZROWS[z]
                dve.wait_ge(rot_in, c * (16 * LOADS) + 16 * LOADS)
                if not first or z >= NZ:
                    dve.wait_ge(pairs_used, c * ZT + (z - NZ + 1))
                nc.vector.tensor_tensor(pairs[0:rows, z % NZ, :], rot[0:rows, z, :], spread[0:rows, :],
                                        ALU.mult).then_inc(pairs_ready, 1)

            def x1_low(c, part):
                cols = slice(0, CHUNK - TILE) if part == 0 else slice(CHUNK - TILE, CHUNK)
                dve.wait_ge(x1h_ready, c * 2 + part + 1)
                nc.vector.tensor_tensor(x1l[:, cols], X1[:, cols], x1h[:, cols].bitcast(fp32),
                                        ALU.subtract).then_inc(x1l_ready, 1)

            def sum_out0(c):
                nc.vector.tensor_reduce(out0[:, bass.ds(c * CB, CB)], X1[:, :].rearrange("p (b d) -> p b d", d=D),
                                        AX.X, ALU.add).then_inc(out0_ready, 1)

            def body(c, first=False, last=False):
                for k in range(TPC):
                    t = c * TPC + k
                    par = k % 2
                    dve.wait_ge(xt_ready, c * 2 + (1 if k < TPC - 1 else 2))
                    if not (first and k < 2):
                        dve.wait_ge(pool_step, x2_count(t - 2))
                    for g in range(NG):
                        if OWNER[g] != "D":
                            continue
                        n = before("D", g)[1]
                        dve.wait_ge(y_done, t * NG + g + 1)
                        for i, f in enumerate(GROUPS[g]):
                            acc = accd[:, par, (n + i) % 2, :]
                            src = Y[(k * NG + g) % NY][:, i * M:(i + 1) * M]
                            if n + i < 2:
                                nc.vector.tensor_scalar(acc, src, x0t[:, k, f:f + 1], None,
                                                        ALU.mult).then_inc(acc_step, 1)
                            else:
                                dve.wait_ge(acc_step, t * DF + n + i - 1)
                                nc.vector.scalar_tensor_tensor(
                                    out=acc, in0=src, scalar=x0t[:, k, f:f + 1], in1=acc,
                                    op0=ALU.mult, op1=ALU.add).then_inc(acc_step, 1)
                        if (k, g) == (0, 0) and not first:
                            x1_low(c, 1)
                        if (k, g) in PAIRS_AT and not last:
                            form_pairs(c + 1, PAIRS_AT[k, g])
                        if (k, g) == (TPC - 1, 2) and not last:
                            x1_low(c + 1, 0)
                        if (k, g) == (TPC - 1, 5) and not last:
                            sum_out0(c + 1)

            nc.vector.memset(diag[:, :, :, :], 0.0).then_inc(diag_clear, 1)
            dve.wait_ge(diag_clear, 1)
            dve.wait_ge(const_in, 16 * CONST_DMAS)
            nc.vector.tensor_copy(diag[:, :, :, F], mask[:, :].rearrange("p (o b) -> p o b", o=1)
                                  .to_broadcast([128, TPC, TB])).then_inc(diag_clear, 1)
            dve.wait_ge(w0_in, 32)
            nc.vector.tensor_tensor(w0[:, :, :].rearrange("p z m -> p (z m)"), w0a, w0b, ALU.add).then_inc(w0_ready, 1)
            for g in range(NG):
                dve.wait_ge(w1h_ready, g + 1)
                nc.vector.tensor_tensor(w1l[:, group_cols(g)], w1raw[:, group_cols(g)],
                                        w1h[:, group_cols(g)].bitcast(fp32), ALU.subtract).then_inc(w1l_ready, 1)
            for z in range(ZT):
                form_pairs(0, z, first=True)
            x1_low(0, 0)
            sum_out0(0)
            x1_low(0, 1)
            chunks(dve, body)
            dve.wait_ge(out2_done, 1)
            nc.vector.tensor_copy(out2[:, :], X1[:, :]).then_inc(out2_ready, 1)
            dve.wait_ge(mlp_in, 16 * MLP_DMAS)
            for m in range(0, H1 // 128, 2):
                dve.wait_ge(h1_done, m + 1)
                nc.vector.tensor_scalar(h1[m], Y[m][:, :], bias1[:, m:m + 1], 0.0, ALU.add,
                                        ALU.max).then_inc(h1_dve, 1)
            dve.wait_ge(h2_done, 1)
            nc.vector.tensor_scalar(h2[0], H2P[0][:, :], bias2[:, 0:1], 0.0, ALU.add, ALU.max).then_inc(h2_dve, 1)
            dve.wait_ge(y_sum, 1)
            nc.vector.tensor_copy(y, MISC[0:1, :]).then_inc(y_ready, 1)

        @block.tensor
        def _(pe):
            def weigh_pairs(c, z, first=False):
                pe.wait_ge(pairs_ready, c * ZT + z + 1)
                if z == 0 and not first:
                    pe.wait_ge(x1l_ready, c * 2)
                rows = ZROWS[z]
                nc.tensor.matmul(X1[:, :], w0[0:rows, z, :], pairs[0:rows, z % NZ, :],
                                 start=(z == 0), stop=(z == ZT - 1)).then_inc(pairs_used, 1)

            def await_x0(c, first=False):
                pe.wait_ge(rot_in, c * (16 * LOADS) + 16 * LOADS)
                if not first:
                    pe.wait_ge(diag_ready, c)

            def turn_x0():
                for k in range(TPC):
                    done = nc.tensor.transpose(XT[:, k, :], spread[0:F, k * TILE:(k + 1) * TILE], ident[0:F, 0:F])
                done.then_inc(xt_done, 1)

            def g_part(t, c, k, first=False):
                pe.wait_ge(pool_step, x2_count(t))
                pe.wait_ge(diag_ready, c + 1)
                if not first:
                    pe.wait_ge(g_stored, t)
                nc.tensor.matmul(MISC[:, 0:FP * TB], x2[:, k % 2, :], diag[:, k, :, :].rearrange("p b f -> p (b f)"),
                                 start=True, stop=True).then_inc(g_done, 1)

            def bank_free(c, k, g, first):
                q = k * NG + g - NY
                if q < 0 and first:
                    return
                t = c * TPC + (q // NG)
                gg = q % NG
                if OWNER[gg] == "D":
                    pe.wait_ge(acc_step, t * DF + (before("D", gg)[1] + len(GROUPS[gg])))
                else:
                    pe.wait_ge(prod_ready, t * AG + (before("A", gg)[0] + 1))

            def body(c, first=False, last=False):
                for k in range(TPC):
                    if k == 0:
                        pe.wait_ge(x1l_ready, c * 2 + 1)
                    if k == TPC - 1:
                        pe.wait_ge(x1l_ready, c * 2 + 2)
                    for g in range(NG):
                        if first and k == 0:
                            pe.wait_ge(w1l_ready, g + 1)
                        if (k, g) == TURN_AT and not last:
                            await_x0(c + 1)
                        bank_free(c, k, g, first)
                        out_y = Y[(k * NG + g) % NY][:, 0:len(GROUPS[g]) * M]
                        cols = group_cols(g)
                        here = slice(k * TILE, (k + 1) * TILE)
                        nc.tensor.matmul(out_y, x1h[:, here], w1h[:, cols], start=True, stop=False)
                        nc.tensor.matmul(out_y, x1h[:, here], w1l[:, cols], start=False, stop=False)
                        nc.tensor.matmul(out_y, x1l[:, here], w1h[:, cols], start=False,
                                         stop=True).then_inc(y_done, 1)
                        if (k, g) in WEIGH_AT and not last:
                            weigh_pairs(c + 1, WEIGH_AT[k, g])
                        if (k, g) == TURN_AT and not last:
                            turn_x0()
                        if g == 8 and not (first and k == 0):
                            if k == 0:
                                g_part(c * TPC - 1, c - 1, TPC - 1)
                            else:
                                g_part(c * TPC + k - 1, c, k - 1, first=first and k == 1)

            pe.wait_ge(const_in, 16 * CONST_DMAS)
            await_x0(0, first=True)
            turn_x0()
            pe.wait_ge(w0_ready, 1)
            for z in range(ZT):
                weigh_pairs(0, z, first=True)
            chunks(pe, body)
            g_part(NT - 1, NCH - 1, TPC - 1)
            pe.wait_ge(w2_in, 16)
            pe.wait_ge(g_stored, NT)
            for f in range(F):
                done = nc.tensor.matmul(X1[:, :], w2[:, f, :], G[:, f, :], start=(f == 0), stop=(f == F - 1))
            done.then_inc(out2_done, 1)
            pe.wait_ge(mlp_in, 16 * MLP_DMAS)
            for part, (rows, src) in enumerate([(M, out0[:, :]), (M, G[:, F, :]), (KD, dense[:, :]),
                                                (M, out2[:, :])]):
                if part == 3:
                    pe.wait_ge(out2_ready, 1)
                kt = [0, 1, 3, 2][part]
                for m in range(H1 // 128):
                    done = nc.tensor.matmul(Y[m][:, :], wt1[0:rows, kt, m * 128:(m + 1) * 128], src,
                                            start=(part == 0), stop=(part == 3))
                    if part == 3:
                        done.then_inc(h1_done, 1)
            for m in range(H2 // 128):
                for kt in range(H1 // 128):
                    if m == 0:
                        if kt % 2:
                            pe.wait_ge(h1_act, kt // 2 + 1)
                        else:
                            pe.wait_ge(h1_dve, kt // 2 + 1)
                    done = nc.tensor.matmul(H2P[m][:, :], wt2[:, kt, m * 128:(m + 1) * 128], h1[kt],
                                            start=(kt == 0), stop=(kt == H1 // 128 - 1))
                done.then_inc(h2_done, 1)
            pe.wait_ge(h2_dve, 1)
            nc.tensor.matmul(MISC[0:1, :], wt3[:, 0:1], h2[0], start=True, stop=False)
            pe.wait_ge(h2_act, 1)
            nc.tensor.matmul(MISC[0:1, :], wt3[:, 1:2], h2[1], start=False, stop=True).then_inc(y_sum, 1)


def constants(np, sizes):
    mask = np.zeros((128, TB), np.float32)
    mask[np.arange(128), np.arange(128) // D] = 1.0
    first = np.cumsum([0] + sizes[:-1]).astype(np.int32)
    return {"c_mask": mask, "c_ident": np.eye(128, dtype=np.float32), "base": np.tile(first, GS).reshape(GROWS, 1)}


def kernel(**inputs):
    import numpy as _np
    import concourse.bacc as _bacc
    from concourse import mybir as _mybir
    from concourse.bass_utils import run_bass_kernel_spmd as _run

    a = {k: _np.asarray(v) for k, v in inputs.items()}
    w0 = a["L0_rec_f0"].reshape(F, F, M)
    w0a = _np.zeros((ZMAX, ZT, M), _np.float32)
    w0b = _np.zeros((ZMAX, ZT, M), _np.float32)
    for s in range(SHIFTS):
        f = _np.arange(F)
        rows = (s % SPT) * F + f
        w0a[rows, s // SPT] = w0[f, (f + s) % F]
        if s:
            w0b[rows, s // SPT] = w0[(f + s) % F, f]
    ids = _np.zeros((GS, F, NCH, GPC), a["ids"].dtype)
    by_chunk = a["ids"].reshape(NCH, CB, F).transpose(2, 0, 1)
    for s in range(GS):
        part = by_chunk[:, :, s * GPC:(s + 1) * GPC]
        ids[s, :, :, 0:part.shape[2]] = part
    tables = [a[f"tbl_{f}"] for f in range(F)]
    arrays = {"tables": _np.concatenate(tables, axis=0)}
    arrays.update(constants(_np, [t.shape[0] for t in tables]))
    arrays.update({
        "ids": ids.reshape(GROWS, NCH * GPC),
        "w0a": w0a.reshape(ZMAX, ZT * M), "w0b": w0b.reshape(ZMAX, ZT * M),
        "w1": a["L0_rec_f1"].reshape(F, M, M).transpose(1, 0, 2).reshape(M, F * M),
        "w2": a["L0_rec_f2"].reshape(F, M, M).transpose(1, 0, 2).reshape(M, F * M),
        "W_top1": a["W_top1"], "W_top2": a["W_top2"],
        "b1": a["b_top1"].reshape(H1 // 128, 128).T, "b2": a["b_top2"].reshape(H2 // 128, 128).T,
        "w3": a["W_top3"].reshape(H2 // 128, 128).T, "dense": a["dense_ctx"].T,
    })
    nc = _bacc.Bacc("TRN2", target_bir_lowering=False, num_devices=1)
    placed, args = {}, {}
    for name, v in arrays.items():
        v = _np.ascontiguousarray(v)
        placed[f"in_{name}"] = v
        args[name] = nc.dram_tensor(f"in_{name}", v.shape, _mybir.dt.from_np(v.dtype), kind="ExternalInput").ap()
    out = nc.dram_tensor("out_y", (B, 1), _mybir.dt.float32, kind="ExternalOutput").ap()
    tower_kernel(nc, args, out)
    r = _run(nc, [placed], core_ids=[0])
    return r.results[0]["out_y"]
```

```python
from contextlib import ExitStack

import concourse.bass as bass
from concourse import mybir

B, F, D, M = 512, 39, 16, 128
FP = F + 1
TILE = 128
TB = TILE // D
TPC = 4
CHUNK = TPC * TILE
CB = CHUNK // D
GS = 3
GPC = -(-CB // GS)
EARLY = 2
GATHERS_AT = [range(2, 5), range(5, 8), range(8, GPC), range(0, EARLY)]
GROWS = GS * F
FULL = CB - (GS - 1) * GPC
NCH = B // CB
NT = NCH * TPC
SHIFTS = F // 2 + 1
SPT = 3
ZT = -(-SHIFTS // SPT)
RP = F + 1
ZROWS = [RP * min(SPT, SHIFTS - SPT * t) for t in range(ZT)]
ZMAX = max(ZROWS)
NZ = 4
FG = 4
GROUPS = [list(range(f, min(f + FG, F))) for f in range(0, F, FG)]
NG = len(GROUPS)
WARM = 12
WARM_AGAIN = 3
HEAD = -(-TB // GS)
TURNS = SPT * (ZT - 1) + ZMAX
W1_PIECES = [range(0, 2), range(2, 6), range(6, 10)]
OWNER = "DADADADADD"
DF = sum(len(g) for g, o in zip(GROUPS, OWNER) if o == "D")
AG = OWNER.count("A")
A_WIDTH = [len(g) * M for g, o in zip(GROUPS, OWNER) if o == "A"]
NY = 5
ROUND = 2 * FG
ROUNDS = -(-F // ROUND)
LAST_ROUND = F - (ROUNDS - 1) * ROUND
H1, H2 = 512, 256
KD = 16
FIRST_LOADS = 3
MID_LOADS = 2
REST_LOADS = ZT + 1 - FIRST_LOADS - MID_LOADS

PAIRS_AT = {(0, 0): 0, (0, 4): 1, (0, 6): 2, (0, 9): 3, (1, 4): 4, (1, 6): 5, (1, 9): 6}
WEIGH_AT = {(0, 6): 0, (0, 9): 1, (1, 2): 2, (1, 5): 3, (1, 9): 4, (2, 2): 5, (2, 5): 6}
MERGE_AT = 0, 4
PAIRS_FIRST = {(1, 4): 0, (1, 6): 1, (1, 8): 2, (1, 9): 3, (2, 2): 4, (2, 4): 5, (2, 6): 6}
WEIGH_FIRST = {(1, 8): 0, (1, 9): 1, (2, 0): 2, (2, 2): 3, (2, 4): 4, (2, 6): 5, (2, 9): 6}
REST_AT = {(0, 4): [0, 1], (0, 6): [2, 3, 4, 5, 6]}
TURN_REST_AT = (0, 7)
WEIGH_REST_AT = {(0, 8): [0, 1], (0, 9): [2, 3, 4, 5, 6]}
G_AT = 9
TURN_AT = (2, 1)


def before(owner, g):
    mine = [GROUPS[i] for i in range(g) if OWNER[i] == owner]
    return len(mine), sum(len(x) for x in mine)


def tower_kernel(nc, args, out):
    fp32, f32r, i32 = mybir.dt.float32, mybir.dt.float32r, mybir.dt.int32
    ALU, ACT, AX = mybir.AluOpType, mybir.ActivationFunctionType, mybir.AxisListType
    ctx = ExitStack()
    with ctx:
        def sb(name, shape, dt=fp32):
            return ctx.enter_context(nc.sbuf_tensor(name, shape, dt))

        def ps(name, cols=512):
            return ctx.enter_context(nc.psum_tensor(name, [128, cols], fp32))

        def sem(name):
            return ctx.enter_context(nc.semaphore(name))

        ident = sb("ident", [128, 128])
        mask = sb("mask", [128, TB])
        base = sb("base", [GROWS, 1], i32)
        w0 = sb("w0", [ZMAX, ZT, M])
        w1h = sb("w1h", [128, F * M], f32r)
        w1l = sb("w1l", [128, F * M], f32r)
        w2 = sb("w2", [128, F, M])
        bias1 = sb("bias1", [128, H1 // 128])
        bias2 = sb("bias2", [128, H2 // 128])
        wt3 = sb("wt3", [128, H2 // 128])
        dense = sb("dense", [KD, B])
        ids_all = sb("ids_all", [GROWS, NCH, GPC], i32)
        rows_all = sb("rows_all", [GROWS, NCH, GPC], i32)
        rows_now = sb("rows_now", [GROWS, GPC], i32)
        rows_b = sb("rows_b", [GROWS, GPC], i32)
        emb = sb("emb", [GROWS, GPC, D])
        emb_b = sb("emb_b", [GROWS, GPC, D])
        x0t = sb("x0t", [128, TPC, F])
        spread = sb("spread", [ZMAX, CHUNK])
        rot = sb("rot", [128, ZT, CHUNK])
        pairs = sb("pairs", [128, NZ, CHUNK])
        x1h = sb("x1h", [128, CHUNK], f32r)
        x1l = sb("x1l", [128, CHUNK], f32r)
        accd = sb("accd", [128, 2, 2, M])
        prod = sb("prod", [128, 2, AG, FG * M])
        sum4 = sb("sum4", [128, FG * M])
        sum2 = sb("sum2", [128, 2 * M])
        sum1 = sb("sum1", [128, 2, M])
        x2 = sb("x2", [128, 2, M])
        diag = sb("diag", [128, TPC, TB, FP])
        G = sb("G", [128, FP, B])
        out0 = sb("out0", [128, B])
        flat = G[:, :, :].rearrange("p f b -> p (f b)")
        w1raw = flat[:, 0:F * M]
        w0a = flat[0:ZMAX, F * M:F * M + ZT * M]
        w0b = flat[0:ZMAX, F * M + ZT * M:F * M + 2 * ZT * M]
        turn_at = F * M + 2 * ZT * M
        turns = flat[0:F, turn_at:turn_at + TURNS + ZMAX]
        turn, same = turns[:, 0:TURNS], turns[:, TURNS:TURNS + ZMAX]
        head = sum1[0:F, 0, :]
        wt1 = rot[:, 0:4, :]
        h1 = [prod[:, m % 2, m // 2, :] for m in range(H1 // 128)]
        wt2 = pairs[:, 0:2, :].rearrange("p a (k n) -> p (a k) n", n=H2)
        h2 = [pairs[:, 2 + m, :] for m in range(H2 // 128)]
        out2 = sum4
        gh = [w1h[:, i * B:(i + 1) * B] for i in range(ROUND)]
        gl = [w1l[:, i * B:(i + 1) * B] for i in range(ROUND)]
        w2h = [x1h, w1h[:, ROUND * B:ROUND * B + FG * M]]
        w2l = [x1l, w1l[:, ROUND * B:ROUND * B + FG * M]]
        y = spread[0:1, :]

        Y = [ps(f"Y{i}") for i in range(NY)]
        X1 = ps("X1")
        MISC = ps("MISC")
        XTB = ps("XTB")
        XT = XTB[:, 0:TPC * F].rearrange("p (k f) -> p k f", k=TPC)
        OUT2P = Y[1]
        H1P = [X1, XTB, Y[0], Y[2]]
        H2P = [Y[3], Y[4]]

        scratch_t = nc.dram_tensor("x0_scratch", (2 * F, CHUNK), fp32)
        scratch = scratch_t.ap()

        ids_in = sem("ids_in")
        const_in = sem("const_in")
        w0_in = sem("w0_in")
        turn_in = sem("turn_in")
        w1_in = [sem(f"w1_in{i}") for i in range(len(W1_PIECES))]
        w2_in = sem("w2_in")
        mlp_in = sem("mlp_in")
        rows_ready = sem("rows_ready")
        rows_set = sem("rows_set")
        emb_in = sem("emb_in")
        emb_b_in = sem("emb_b_in")
        head_in = sem("head_in")
        head_done = sem("head_done")
        head_ready = sem("head_ready")
        head_spread_done = sem("head_spread_done")
        head_spread_ready = sem("head_spread_ready")
        head_turned = sem("head_turned")
        head_pairs = sem("head_pairs")
        head_x1_done = sem("head_x1_done")
        head_x1h_ready = sem("head_x1h_ready")
        head_x1l_ready = sem("head_x1l_ready")
        head_xt_done = sem("head_xt_done")
        head_xt_ready = sem("head_xt_ready")
        scratch_in = sem("scratch_in")
        first_in = sem("first_in")
        mid_in = sem("mid_in")
        rest_in = sem("rest_in")
        w0_ready = sem("w0_ready")
        w1h_ready = sem("w1h_ready")
        w1l_ready = sem("w1l_ready")
        diag_clear = sem("diag_clear")
        pairs_ready = sem("pairs_ready")
        pairs_used = sem("pairs_used")
        xt_done = sem("xt_done")
        xt_ready = sem("xt_ready")
        diag_ready = sem("diag_ready")
        x1h_ready = sem("x1h_ready")
        x1l_ready = sem("x1l_ready")
        out0_ready = sem("out0_ready")
        y_done = sem("y_done")
        acc_step = sem("acc_step")
        prod_ready = sem("prod_ready")
        pool_step = sem("pool_step")
        pair_summed = sem("pair_summed")
        x2_ready = sem("x2_ready")
        g_done = sem("g_done")
        g_stored = sem("g_stored")
        gh_ready = sem("gh_ready")
        gl_ready = sem("gl_ready")
        w2h_ready = sem("w2h_ready")
        w2l_ready = sem("w2l_ready")
        g_used = sem("g_used")
        out2_ready = sem("out2_ready")
        h1_done = sem("h1_done")
        h1_act = sem("h1_act")
        h1_dve = sem("h1_dve")
        h2_done = sem("h2_done")
        h2_act = sem("h2_act")
        h2_dve = sem("h2_dve")
        y_sum = sem("y_sum")
        y_ready = sem("y_ready")
        stored = sem("stored")

        POOL_STEPS = AG + 1
        CONST_DMAS, MLP_DMAS = 2, 7

        def summed(t):
            return POOL_STEPS * t + POOL_STEPS

        def chunks(eng, body):
            body(0, first=True)
            with eng.Fori(1, NCH - 1) as c:
                body(c)
            body(NCH - 1, last=True)

        def rounds(eng, body):
            body(0, ROUND, first=True)
            with eng.Fori(1, ROUNDS - 1) as r:
                body(r, ROUND)
            body(ROUNDS - 1, LAST_ROUND, last=True)

        def group_cols(g):
            return slice(g * FG * M, min((g + 1) * FG, F) * M)

        block = ctx.enter_context(nc.Block())

        @block.sync
        def _(sp):
            def store_x0(where, before=None):
                if before is not None:
                    sp.wait_ge(first_in, before * (16 * FIRST_LOADS) + 16 * FIRST_LOADS)
                    sp.wait_ge(mid_in, before * (16 * MID_LOADS) + 16 * MID_LOADS)
                    sp.wait_ge(rest_in, before * (16 * REST_LOADS) + 16 * REST_LOADS)
                for s in range(GS):
                    n = GPC if s < GS - 1 else FULL
                    src = where[s * F:(s + 1) * F, 0:n, :].rearrange("f (o i) d -> f o (i d)", o=1)
                    sp.dma_start(bass.AP(tensor=scratch_t, offset=s * GPC * D,
                                         ap=[[CHUNK, F], [F * CHUNK, 2], [1, n * D]]),
                                 src.to_broadcast([F, 2, n * D])).then_inc(scratch_in, 16)

            def store_rest():
                for s in range(GS):
                    src = emb[s * F:(s + 1) * F, HEAD:GPC, :].rearrange("f (o i) d -> f o (i d)", o=1)
                    sp.dma_start(bass.AP(tensor=scratch_t, offset=(s + 1) * TILE,
                                         ap=[[CHUNK, F], [F * CHUNK, 2], [1, TILE]]),
                                 src.to_broadcast([F, 2, TILE])).then_inc(scratch_in, 16)

            def load_x0(c, before=None):
                sp.wait_ge(scratch_in, c * (16 * GS) + 16 * GS)
                lo = TILE if before is None else 0
                if before is not None:
                    sp.wait_ge(pairs_ready, before * ZT + ZT)
                    sp.wait_ge(xt_done, c)
                sp.dma_start(spread[:, lo:CHUNK],
                             bass.AP(tensor=scratch_t, offset=lo, ap=[[0, SPT], [CHUNK, RP], [1, CHUNK - lo]])
                             ).then_inc(first_in, 16)
                for z in range(ZT):
                    sp.dma_start(rot[0:ZROWS[z], z, lo:CHUNK],
                                 bass.AP(tensor=scratch_t, offset=SPT * z * CHUNK + lo,
                                         ap=[[CHUNK, ZROWS[z] // RP], [CHUNK, RP], [1, CHUNK - lo]])
                                 ).then_inc(first_in if z < FIRST_LOADS - 1 else
                                            mid_in if z < FIRST_LOADS - 1 + MID_LOADS else rest_in, 16)

            sp.dma_start(ids_all[:, :, :].rearrange("p c i -> p (c i)"), args["ids"]).then_inc(ids_in, 16)
            sp.dma_start(base[:, :], args["base"]).then_inc(ids_in, 16)
            sp.dma_start(turns, args["c_turn"]).then_inc(turn_in, 16)
            sp.dma_start(ident[:, :], args["c_ident"]).then_inc(const_in, 16)
            sp.dma_start(mask[:, :], args["c_mask"]).then_inc(const_in, 16)
            sp.dma_start(w0a, args["w0a"]).then_inc(w0_in, 16)
            sp.dma_start(w0b, args["w0b"]).then_inc(w0_in, 16)
            for i, groups in enumerate(W1_PIECES):
                if i == 1:
                    sp.wait_ge(head_in, 16 * HEAD)
                cols = slice(group_cols(groups[0]).start, group_cols(groups[-1]).stop)
                sp.dma_start(w1raw[:, cols], args["w1"][:, cols]).then_inc(w1_in[i], 16)
            sp.wait_ge(emb_in, 16 * (GPC - HEAD))
            store_rest()
            load_x0(0)
            sp.wait_ge(emb_b_in, 16 * GPC)
            store_x0(emb_b, before=0)
            load_x0(1, before=0)
            sp.dma_start(w2[:, :, :].rearrange("p f m -> p (f m)"), args["w2"]).then_inc(w2_in, 16)
            with sp.Fori(1, NCH - 1) as c:
                sp.wait_ge(emb_in, c * (16 * GPC) + 16 * (GPC - HEAD))
                store_x0(emb, before=c)
                load_x0(c + 1, before=c)
            sp.dma_start(bias1[:, :], args["b1"]).then_inc(mlp_in, 16)
            sp.dma_start(bias2[:, :], args["b2"]).then_inc(mlp_in, 16)
            sp.dma_start(wt3[:, :], args["w3"]).then_inc(mlp_in, 16)
            sp.dma_start(dense[:, :], args["dense"]).then_inc(mlp_in, 16)
            sp.wait_ge(pairs_used, NCH * ZT)
            w_top1 = args["W_top1"]
            sp.dma_start(wt1[:, 0:3, :], w_top1[0:3 * M, :].rearrange("(k p) n -> p k n", p=128)).then_inc(mlp_in, 16)
            sp.dma_start(wt1[0:KD, 3, :], w_top1[3 * M:3 * M + KD, :]).then_inc(mlp_in, 16)
            sp.dma_start(wt2, args["W_top2"].rearrange("(k p) n -> p k n", p=128)).then_inc(mlp_in, 16)
            sp.wait_ge(y_ready, 1)
            sp.dma_start(out.rearrange("b o -> o b"), y).then_inc(stored, 16)
            sp.wait_ge(stored, 16)

        @block.gpsimd
        def _(pool):
            def set_rows(c, where, first=False):
                if not first:
                    pool.wait_ge(emb_in, c * (16 * GPC) - 16 * (GPC + HEAD))
                    pool.wait_ge(scratch_in, c * (16 * GS))
                nc.gpsimd.tensor_copy(where[:, :], rows_all[:, bass.ds(c, 1), :].rearrange("p o i -> p (o i)")
                                      ).then_inc(rows_set, 1)

            def gather(i, rows, to, landed, short=FULL):
                n = GROWS if i != short else GROWS - F
                nc.gpsimd.indirect_dma_start(
                    out=to[0:n, i, :], out_offset=None, in_=args["tables"],
                    in_offset=bass.IndirectOffsetOnAxis(ap=rows[0:n, i:i + 1], axis=0)).then_inc(landed, 16)

            def body(c, first=False, gathers=(True, True)):
                for k in range(TPC):
                    t = c * TPC + k
                    par = k % 2
                    fresh = first and k < 2
                    pool.wait_ge(prod_ready, t * AG + 2)
                    nc.gpsimd.tensor_tensor(sum4[:, :], prod[:, par, 0, :], prod[:, par, 1, :],
                                            ALU.add).then_inc(pool_step, 1)
                    if k < TPC - 1 and gathers[0] and not (first and k == 0):
                        for i in GATHERS_AT[k]:
                            gather(i, rows_now, emb, emb_in)
                    for a in range(2, AG):
                        n = A_WIDTH[a]
                        pool.wait_ge(prod_ready, t * AG + a + 1)
                        pool.wait_ge(pool_step, t * POOL_STEPS + a - 1)
                        nc.gpsimd.tensor_tensor(sum4[:, 0:n], sum4[:, 0:n], prod[:, par, a, 0:n],
                                                ALU.add).then_inc(pool_step, 1)
                    pool.wait_ge(pool_step, t * POOL_STEPS + AG - 1)
                    nc.gpsimd.tensor_tensor(sum2[:, :], sum4[:, 0:2 * M], sum4[:, 2 * M:4 * M],
                                            ALU.add).then_inc(pool_step, 1)
                    if k == TPC - 1 and gathers[1]:
                        set_rows(c + 3, rows_now)
                        pool.wait_ge(rows_set, c + 4)
                    if first and k == 0:
                        pool.wait_ge(scratch_in, 16 * GS)
                        pool.wait_ge(head_done, 1)
                        set_rows(2, rows_now, first=True)
                        pool.wait_ge(rows_set, 3)
                    pool.wait_ge(pool_step, t * POOL_STEPS + AG)
                    if not fresh:
                        pool.wait_ge(x2_ready, t - 1)
                    nc.gpsimd.tensor_tensor(sum1[:, par, :], sum2[:, 0:M], sum2[:, M:2 * M],
                                            ALU.add).then_inc(pool_step, 1)
                    if k == TPC - 1 and gathers[1]:
                        for i in GATHERS_AT[k]:
                            gather(i, rows_now, emb, emb_in)
                    if first and k == 0:
                        for i in range(0, GATHERS_AT[0].stop):
                            gather(i, rows_now, emb, emb_in)

            pool.wait_ge(ids_in, 32)
            nc.gpsimd.tensor_tensor(rows_all[:, :, :].rearrange("p c i -> p (c i)"),
                                    ids_all[:, :, :].rearrange("p c i -> p (c i)"),
                                    base[:, :].to_broadcast([GROWS, NCH * GPC]), ALU.add).then_inc(rows_ready, 1)
            pool.wait_ge(rows_ready, 1)
            set_rows(0, rows_now, first=True)
            set_rows(1, rows_b, first=True)
            pool.wait_ge(rows_set, 2)
            for i in range(GPC):
                gather(i, rows_now, emb, head_in if i < HEAD else emb_in, short=HEAD - 1)
            for i in range(GPC):
                gather(i, rows_b, emb_b, emb_b_in)
            body(0, first=True)
            with pool.Fori(1, NCH - 3) as c:
                body(c)
            body(NCH - 3, gathers=(True, False))
            with pool.Fori(NCH - 2, NCH) as c:
                body(c, gathers=(False, False))

            for b, groups in enumerate(GROUPS):
                cols = len(groups) * M
                pool.wait_ge(w2h_ready, b + 1)
                nc.gpsimd.tensor_tensor(w2l[b % 2][:, 0:cols],
                                        w2[:, groups[0]:groups[-1] + 1, :].rearrange("p f m -> p (f m)"),
                                        w2h[b % 2][:, 0:cols].bitcast(fp32), ALU.subtract).then_inc(w2l_ready, 1)

        @block.scalar
        def _(act):
            def keep_xt(c, part):
                tiles = slice(0, TPC - 1) if part == 0 else slice(TPC - 1, TPC)
                act.wait_ge(xt_done, c + 1)
                nc.scalar.copy(x0t[:, tiles, :], XT[:, tiles, :]).then_inc(xt_ready, 1)

            def fill_diag(half):
                for b in range(half * TB // 2, (half + 1) * TB // 2):
                    rows = slice(b * D // 32 * 32, b * D // 32 * 32 + 32)
                    done = nc.scalar.activation(diag[rows, :, b, 0:F], XT[rows, :, :], ACT.Copy,
                                                scale=mask[rows, b:b + 1])
                if half:
                    done.then_inc(diag_ready, 1)

            def x1_high(c, part):
                cols = slice(0, CHUNK - TILE) if part == 0 else slice(CHUNK - TILE, CHUNK)
                act.wait_ge(pairs_used, c * ZT + ZT)
                if part == 1:
                    act.wait_ge(out0_ready, c + 1)
                nc.scalar.copy(x1h[:, cols], X1[:, cols]).then_inc(x1h_ready, 1)

            def store_g(t):
                act.wait_ge(g_done, t + 1)
                nc.scalar.copy(G[:, :, bass.ds(t * TB, TB)].rearrange("p f b -> p b f"),
                               MISC[:, 0:FP * TB].rearrange("p (b f) -> p b f", f=FP)).then_inc(g_stored, 1)

            def body(c, first=False, last=False):
                for k in range(TPC):
                    t = c * TPC + k
                    par = k % 2
                    if k == 0 and not first:
                        act.wait_ge(y_done, t * NG)
                        x1_high(c, 1)
                    if k == TPC - 1 and not last:
                        act.wait_ge(y_done, t * NG)
                        x1_high(c + 1, 0)
                    if not (first and k < 2):
                        store_g(t - 2)
                    for g in range(NG):
                        if OWNER[g] != "A":
                            continue
                        a = before("A", g)[0]
                        if a == 0:
                            if first and k == 0:
                                act.wait_ge(head_xt_ready, 1)
                            else:
                                act.wait_ge(xt_ready, c * 2 + (1 if k < TPC - 1 else 2))
                            if not (first and k < 2):
                                act.wait_ge(pool_step, summed(t - 2))
                        act.wait_ge(y_done, t * NG + g + 1)
                        for i, f in enumerate(GROUPS[g]):
                            done = nc.scalar.activation(
                                prod[:, par, a, i * M:(i + 1) * M], Y[(k * NG + g) % NY][:, i * M:(i + 1) * M],
                                ACT.Copy, scale=x0t[:, k, f:f + 1])
                        done.then_inc(prod_ready, 1)
                        if a == 0 and k == 0 and not first:
                            act.wait_ge(acc_step, t * DF)
                            act.wait_ge(prod_ready, t * AG)
                            keep_xt(c, 1)
                        if a < 2 and k == 1 and not first:
                            fill_diag(a)
                        if a == AG - 1 and k == 0 and first:
                            rest_of_chunk0()
                        if a == 1 and k == TPC - 1 and not last:
                            act.wait_ge(acc_step, t * DF)
                            act.wait_ge(prod_ready, t * AG)
                            keep_xt(c + 1, 0)

            def w1_high(groups):
                for g in groups:
                    nc.scalar.copy(w1h[:, group_cols(g)], w1raw[:, group_cols(g)]).then_inc(w1h_ready, 1)

            def rest_of_chunk0():
                act.wait_ge(xt_done, 1)
                nc.scalar.copy(x0t[:, 1:TPC, :], XT[:, 1:TPC, :]).then_inc(xt_ready, 2)
                act.wait_ge(diag_clear, 2)
                fill_diag(0)
                fill_diag(1)
                act.wait_ge(pairs_used, ZT)
                nc.scalar.copy(x1h[:, TILE:CHUNK], X1[:, TILE:CHUNK]).then_inc(x1h_ready, 2)

            act.wait_ge(w1_in[0], 16)
            w1_high(W1_PIECES[0])
            act.wait_ge(head_done, 1)
            nc.scalar.copy(head, MISC[0:F, TILE:2 * TILE]).then_inc(head_ready, 1)
            act.wait_ge(head_spread_done, 1)
            nc.scalar.copy(spread[:, 0:TILE], MISC[0:ZMAX, 0:TILE]).then_inc(head_spread_ready, 1)
            act.wait_ge(head_xt_done, 1)
            nc.scalar.copy(x0t[:, 0, :], XT[:, 0, :]).then_inc(head_xt_ready, 1)
            act.wait_ge(w1_in[1], 16)
            w1_high(W1_PIECES[1])
            act.wait_ge(head_x1_done, 1)
            nc.scalar.copy(x1h[:, 0:TILE], X1[:, 0:TILE]).then_inc(head_x1h_ready, 1)
            act.wait_ge(w1_in[2], 16)
            w1_high(W1_PIECES[2])
            chunks(act, body)
            store_g(NT - 2)
            store_g(NT - 1)

            def highs(r, n, first=False, last=False):
                for i in range(n):
                    if i % FG == 0:
                        cols = min(FG, n - i) * M
                        if not first:
                            act.wait_ge(g_used, r * ROUND + (i + FG - ROUND))
                        nc.scalar.copy(w2h[i // FG][:, 0:cols], w2[:, bass.ds(r * ROUND + i, cols // M), :]
                                       .rearrange("p f m -> p (f m)")).then_inc(w2h_ready, 1)
                    if not first:
                        act.wait_ge(g_used, r * ROUND + (i + 1 - ROUND))
                    nc.scalar.copy(gh[i], G[:, bass.ds(r * ROUND + i, 1), :].rearrange("p f b -> p (f b)")
                                   ).then_inc(gh_ready, 1)

            act.wait_ge(w2_in, 16)
            act.wait_ge(g_stored, NT)
            rounds(act, highs)
            act.wait_ge(mlp_in, 16 * MLP_DMAS)
            for m in range(1, H1 // 128, 2):
                act.wait_ge(h1_done, m + 1)
                nc.scalar.activation(h1[m], H1P[m][:, :], ACT.Relu, bias=bias1[:, m:m + 1]).then_inc(h1_act, 1)
            act.wait_ge(h2_done, 2)
            nc.scalar.activation(h2[1], H2P[1][:, :], ACT.Relu, bias=bias2[:, 1:2]).then_inc(h2_act, 1)

        @block.vector
        def _(dve):
            def form_pairs(c, z, first=False):
                rows = ZROWS[z]
                if z < FIRST_LOADS - 1:
                    dve.wait_ge(first_in, c * (16 * FIRST_LOADS) + 16 * FIRST_LOADS)
                elif z < FIRST_LOADS - 1 + MID_LOADS:
                    dve.wait_ge(mid_in, c * (16 * MID_LOADS) + 16 * MID_LOADS)
                else:
                    dve.wait_ge(rest_in, c * (16 * REST_LOADS) + 16 * REST_LOADS)
                if not first or z >= NZ:
                    dve.wait_ge(pairs_used, c * ZT + (z - NZ + 1))
                cols = slice(TILE if first else 0, CHUNK)
                nc.vector.tensor_tensor(pairs[0:rows, z % NZ, cols], rot[0:rows, z, cols], spread[0:rows, cols],
                                        ALU.mult).then_inc(pairs_ready, 1)

            def x1_low(c, part):
                cols = slice(0, CHUNK - TILE) if part == 0 else slice(CHUNK - TILE, CHUNK)
                dve.wait_ge(x1h_ready, c * 2 + part + 1)
                nc.vector.tensor_tensor(x1l[:, cols], X1[:, cols], x1h[:, cols].bitcast(fp32),
                                        ALU.subtract).then_inc(x1l_ready, 1)

            def sum_out0(c):
                nc.vector.tensor_reduce(out0[:, bass.ds(c * CB, CB)], X1[:, :].rearrange("p (b d) -> p b d", d=D),
                                        AX.X, ALU.add).then_inc(out0_ready, 1)

            def merge_own(t, par):
                dve.wait_ge(acc_step, t * DF + DF)
                nc.vector.tensor_tensor(accd[:, par, 0, :], accd[:, par, 0, :], accd[:, par, 1, :],
                                        ALU.add).then_inc(pair_summed, 1)

            def merge_x2(t, par, fresh=False):
                dve.wait_ge(pair_summed, t + 1)
                dve.wait_ge(pool_step, summed(t))
                if not fresh:
                    dve.wait_ge(g_done, t - 1)
                nc.vector.tensor_tensor(x2[:, par, :], accd[:, par, 0, :], sum1[:, par, :],
                                        ALU.add).then_inc(x2_ready, 1)

            def body(c, first=False, last=False):
                for k in range(TPC):
                    t = c * TPC + k
                    par = k % 2
                    if first and k == 0:
                        dve.wait_ge(head_xt_ready, 1)
                    else:
                        dve.wait_ge(xt_ready, c * 2 + (1 if k < TPC - 1 else 2))
                    if not (first and k < 2):
                        dve.wait_ge(x2_ready, t - 1)
                    for g in range(NG):
                        if OWNER[g] != "D":
                            continue
                        n = before("D", g)[1]
                        dve.wait_ge(y_done, t * NG + g + 1)
                        for i, f in enumerate(GROUPS[g]):
                            acc = accd[:, par, (n + i) % 2, :]
                            src = Y[(k * NG + g) % NY][:, i * M:(i + 1) * M]
                            if n + i < 2:
                                nc.vector.tensor_scalar(acc, src, x0t[:, k, f:f + 1], None,
                                                        ALU.mult).then_inc(acc_step, 1)
                            else:
                                dve.wait_ge(acc_step, t * DF + n + i - 1)
                                nc.vector.scalar_tensor_tensor(
                                    out=acc, in0=src, scalar=x0t[:, k, f:f + 1], in1=acc,
                                    op0=ALU.mult, op1=ALU.add).then_inc(acc_step, 1)
                        if g == MERGE_AT[0] and not (first and k == 0):
                            merge_own(t - 1, 1 - par)
                        if g == MERGE_AT[1] and not (first and k == 0):
                            merge_x2(t - 1, 1 - par, fresh=first and k < 3)
                        if (k, g) == (0, 0) and not first:
                            x1_low(c, 1)
                        pairs_at = PAIRS_FIRST if first else PAIRS_AT
                        if (k, g) in pairs_at and not last:
                            form_pairs(c + 1, pairs_at[k, g])
                        if (k, g) == (TPC - 1, 2) and not last:
                            x1_low(c + 1, 0)
                        if (k, g) == (TPC - 1, 6) and not last:
                            sum_out0(c + 1)
                        if first and (k, g) in REST_AT:
                            for z in REST_AT[k, g]:
                                form_pairs(0, z, first=True)
                    if first and k == 0:
                        rest_of_chunk0()

            def w1_low(groups):
                for g in groups:
                    dve.wait_ge(w1h_ready, g + 1)
                    nc.vector.tensor_tensor(w1l[:, group_cols(g)], w1raw[:, group_cols(g)],
                                            w1h[:, group_cols(g)].bitcast(fp32), ALU.subtract).then_inc(w1l_ready, 1)

            def head_products(bank, zs, at):
                n = len(zs)
                nc.vector.tensor_tensor(
                    pairs[0:ZMAX, 0:n, at:at + TILE],
                    Y[bank][0:ZMAX, 0:n * TILE].rearrange("p (z c) -> p z c", z=n),
                    spread[:, 0:TILE].rearrange("p (o c) -> p o c", o=1).to_broadcast([ZMAX, n, TILE]),
                    ALU.mult).then_inc(head_pairs, 1)

            def rest_of_chunk0():
                dve.wait_ge(x1h_ready, 2)
                nc.vector.tensor_tensor(x1l[:, TILE:CHUNK], X1[:, TILE:CHUNK], x1h[:, TILE:CHUNK].bitcast(fp32),
                                        ALU.subtract).then_inc(x1l_ready, 2)
                sum_out0(0)

            nc.vector.memset(diag[:, :, :, :], 0.0).then_inc(diag_clear, 1)
            dve.wait_ge(diag_clear, 1)
            dve.wait_ge(const_in, 16 * CONST_DMAS)
            nc.vector.tensor_copy(diag[:, :, :, F], mask[:, :].rearrange("p (o b) -> p o b", o=1)
                                  .to_broadcast([128, TPC, TB])).then_inc(diag_clear, 1)
            dve.wait_ge(w0_in, 32)
            nc.vector.tensor_tensor(w0[:, :, :].rearrange("p z m -> p (z m)"), w0a, w0b, ALU.add).then_inc(w0_ready, 1)
            w1_low(W1_PIECES[0])
            dve.wait_ge(head_spread_ready, 1)
            dve.wait_ge(head_turned, 1)
            head_products(0, range(0, NZ), 0)
            dve.wait_ge(head_turned, 2)
            head_products(1, range(NZ, ZT), TILE)
            w1_low(W1_PIECES[1][:2])
            dve.wait_ge(head_x1h_ready, 1)
            nc.vector.tensor_tensor(x1l[:, 0:TILE], X1[:, 0:TILE], x1h[:, 0:TILE].bitcast(fp32),
                                    ALU.subtract).then_inc(head_x1l_ready, 1)
            w1_low(W1_PIECES[1][2:])
            w1_low(W1_PIECES[2])
            chunks(dve, body)
            merge_own(NT - 1, (NT - 1) % 2)
            merge_x2(NT - 1, (NT - 1) % 2)

            def g_low(r, n, first=False, last=False):
                for i in range(n):
                    dve.wait_ge(gh_ready, r * ROUND + (i + 1))
                    nc.vector.tensor_tensor(gl[i], G[:, bass.ds(r * ROUND + i, 1), :].rearrange("p f b -> p (f b)"),
                                            gh[i].bitcast(fp32), ALU.subtract).then_inc(gl_ready, 1)

            rounds(dve, g_low)
            dve.wait_ge(g_used, F)
            nc.vector.tensor_copy(out2[:, :], OUT2P[:, :]).then_inc(out2_ready, 1)
            dve.wait_ge(mlp_in, 16 * MLP_DMAS)
            for m in range(0, H1 // 128, 2):
                dve.wait_ge(h1_done, m + 1)
                nc.vector.tensor_scalar(h1[m], H1P[m][:, :], bias1[:, m:m + 1], 0.0, ALU.add,
                                        ALU.max).then_inc(h1_dve, 1)
            dve.wait_ge(h2_done, 1)
            nc.vector.tensor_scalar(h2[0], H2P[0][:, :], bias2[:, 0:1], 0.0, ALU.add, ALU.max).then_inc(h2_dve, 1)
            dve.wait_ge(y_sum, 1)
            nc.vector.tensor_copy(y, MISC[0:1, :]).then_inc(y_ready, 1)

        @block.tensor
        def _(pe):
            def weigh_pairs(c, z, first=False):
                pe.wait_ge(pairs_ready, c * ZT + z + 1)
                if z == 0 and not first:
                    pe.wait_ge(x1l_ready, c * 2)
                rows = ZROWS[z]
                cols = slice(TILE if first else 0, CHUNK)
                nc.tensor.matmul(X1[:, cols], w0[0:rows, z, :], pairs[0:rows, z % NZ, cols],
                                 start=(z == 0), stop=(z == ZT - 1)).then_inc(pairs_used, 1)

            def await_x0(c, first=False):
                pe.wait_ge(first_in, c * (16 * FIRST_LOADS) + 16 * FIRST_LOADS)
                if not first:
                    pe.wait_ge(diag_ready, c)

            def turn_x0(tiles=range(TPC)):
                for k in tiles:
                    done = nc.tensor.transpose(XT[:, k, :], spread[0:F, k * TILE:(k + 1) * TILE], ident[0:F, 0:F])
                done.then_inc(xt_done, 1)

            def g_part(t, c, k, first=False):
                pe.wait_ge(x2_ready, t + 1)
                pe.wait_ge(diag_ready, c + 1)
                if not first:
                    pe.wait_ge(g_stored, t)
                nc.tensor.matmul(MISC[:, 0:FP * TB], x2[:, k % 2, :], diag[:, k, :, :].rearrange("p b f -> p (b f)"),
                                 start=True, stop=True).then_inc(g_done, 1)

            def bank_free(c, k, g, first):
                q = k * NG + g - NY
                if q < 0 and first:
                    return
                t = c * TPC + (q // NG)
                gg = q % NG
                if OWNER[gg] == "D":
                    pe.wait_ge(acc_step, t * DF + (before("D", gg)[1] + len(GROUPS[gg])))
                else:
                    pe.wait_ge(prod_ready, t * AG + (before("A", gg)[0] + 1))

            def body(c, first=False, last=False):
                for k in range(TPC):
                    if first and k == 0:
                        pe.wait_ge(head_x1l_ready, 1)
                    elif k == (1 if first else 0):
                        pe.wait_ge(x1l_ready, c * 2 + 1)
                    if k == TPC - 1:
                        pe.wait_ge(x1l_ready, c * 2 + 2)
                    for g in range(NG):
                        if first and k == 0:
                            pe.wait_ge(w1l_ready, g + 1)
                        if (k, g) == TURN_AT and not last:
                            await_x0(c + 1)
                        bank_free(c, k, g, first)
                        out_y = Y[(k * NG + g) % NY][:, 0:len(GROUPS[g]) * M]
                        cols = group_cols(g)
                        here = slice(k * TILE, (k + 1) * TILE)
                        nc.tensor.matmul(out_y, x1h[:, here], w1h[:, cols], start=True, stop=False)
                        nc.tensor.matmul(out_y, x1h[:, here], w1l[:, cols], start=False, stop=False)
                        nc.tensor.matmul(out_y, x1l[:, here], w1h[:, cols], start=False,
                                         stop=True).then_inc(y_done, 1)
                        weigh_at = WEIGH_FIRST if first else WEIGH_AT
                        if (k, g) in weigh_at and not last:
                            weigh_pairs(c + 1, weigh_at[k, g])
                        if (k, g) == TURN_AT and not last:
                            turn_x0()
                        if g == G_AT and not (first and k == 0):
                            if k == 0:
                                g_part(c * TPC - 1, c - 1, TPC - 1)
                            else:
                                g_part(c * TPC + k - 1, c, k - 1, first=first and k == 1)
                        if first and (k, g) == TURN_REST_AT:
                            turn_rest()
                        if first and (k, g) in WEIGH_REST_AT:
                            for z in WEIGH_REST_AT[k, g]:
                                weigh_pairs(0, z, first=True)

            def collect_head():
                for s in range(GS):
                    rows, n = (F * (GS - 1), HEAD) if s < GS - 1 else (GROWS, HEAD - 1)
                    to = TILE + s * HEAD * D
                    done = nc.tensor.matmul(MISC[0:F, to:to + n * D], ident[0:rows, s * F:(s + 1) * F],
                                            emb[0:rows, 0:n, :].rearrange("p i d -> p (i d)"), start=True, stop=True)
                done.then_inc(head_done, 1)

            def turn_rest():
                await_x0(0, first=True)
                pe.wait_ge(head_xt_ready, 1)
                turn_x0(range(1, TPC))

            pe.wait_ge(const_in, 16 * CONST_DMAS)
            for i in range(WARM):
                nc.tensor.matmul(Y[0][:, 0:128], ident[:, :], ident[:, :], start=True, stop=True)
            pe.wait_ge(head_in, 16 * HEAD)
            collect_head()
            pe.wait_ge(turn_in, 16)
            pe.wait_ge(head_ready, 1)
            nc.tensor.matmul(MISC[0:ZMAX, 0:TILE], same, head, start=True, stop=True).then_inc(head_spread_done, 1)
            for z in range(ZT):
                at = z % NZ * TILE
                done = nc.tensor.matmul(Y[z // NZ][0:ZMAX, at:at + TILE], turn[:, SPT * z:SPT * z + ZMAX], head,
                                        start=True, stop=True)
                if z in (NZ - 1, ZT - 1):
                    done.then_inc(head_turned, 1)
            pe.wait_ge(head_spread_ready, 1)
            nc.tensor.transpose(XT[:, 0, :], spread[0:F, 0:TILE], ident[0:F, 0:F]).then_inc(head_xt_done, 1)
            pe.wait_ge(w0_ready, 1)
            for z in range(ZT):
                if z % NZ == 0:
                    pe.wait_ge(head_pairs, z // NZ + 1)
                at = z // NZ * TILE
                done = nc.tensor.matmul(X1[:, 0:TILE], w0[0:ZROWS[z], z, :], pairs[0:ZROWS[z], z % NZ, at:at + TILE],
                                        start=(z == 0), stop=(z == ZT - 1))
            done.then_inc(head_x1_done, 1)
            for i in range(WARM_AGAIN):
                nc.tensor.matmul(Y[2][:, 0:128], ident[:, :], ident[:, :], start=True, stop=True)
            chunks(pe, body)

            def first_layer(part, m):
                rows, src, kt = [(M, out0[:, :], 0), (KD, dense[:, :], 3), (M, G[:, F, :], 1), (M, out2[:, :], 2)][part]
                return nc.tensor.matmul(H1P[m][:, :], wt1[0:rows, kt, m * 128:(m + 1) * 128], src,
                                        start=(part == 0), stop=(part == 3))

            pe.wait_ge(mlp_in, 16 * MLP_DMAS)
            pe.wait_ge(out0_ready, NCH)
            for m in (0, 1):
                first_layer(0, m)
                first_layer(1, m)
            g_part(NT - 1, NCH - 1, TPC - 1)
            pe.wait_ge(prod_ready, NT * AG)
            pe.wait_ge(acc_step, NT * DF)
            first_layer(0, 2)
            first_layer(1, 2)
            first_layer(0, 3)
            first_layer(1, 3)
            pe.wait_ge(g_stored, NT)
            for m in (0, 1):
                first_layer(2, m)

            def weigh_g(r, n, first=False, last=False):
                for i in range(n):
                    if i % FG == 0:
                        pe.wait_ge(w2l_ready, r * (ROUND // FG) + (i // FG + 1))
                    pe.wait_ge(gl_ready, r * ROUND + (i + 1))
                    at = slice(i % FG * M, (i % FG + 1) * M)
                    high, low = w2h[i // FG][:, at], w2l[i // FG][:, at]
                    nc.tensor.matmul(OUT2P[:, :], high, gh[i], start=(first and i == 0), stop=False)
                    nc.tensor.matmul(OUT2P[:, :], low, gh[i], start=False, stop=False)
                    nc.tensor.matmul(OUT2P[:, :], high, gl[i], start=False,
                                     stop=(last and i == n - 1)).then_inc(g_used, 1)

            rounds(pe, weigh_g)
            for m in (2, 3):
                first_layer(2, m)
            pe.wait_ge(out2_ready, 1)
            for m in range(H1 // 128):
                first_layer(3, m).then_inc(h1_done, 1)
            for m in range(H2 // 128):
                for kt in range(H1 // 128):
                    if m == 0:
                        if kt % 2:
                            pe.wait_ge(h1_act, kt // 2 + 1)
                        else:
                            pe.wait_ge(h1_dve, kt // 2 + 1)
                    done = nc.tensor.matmul(H2P[m][:, :], wt2[:, kt, m * 128:(m + 1) * 128], h1[kt],
                                            start=(kt == 0), stop=(kt == H1 // 128 - 1))
                done.then_inc(h2_done, 1)
            pe.wait_ge(h2_dve, 1)
            nc.tensor.matmul(MISC[0:1, :], wt3[:, 0:1], h2[0], start=True, stop=False)
            pe.wait_ge(h2_act, 1)
            nc.tensor.matmul(MISC[0:1, :], wt3[:, 1:2], h2[1], start=False, stop=True).then_inc(y_sum, 1)


def constants(np, sizes):
    mask = np.zeros((128, TB), np.float32)
    mask[np.arange(128), np.arange(128) // D] = 1.0
    first = np.cumsum([0] + sizes[:-1]).astype(np.int32)
    c_turn = np.zeros((F, TURNS + ZMAX), np.float32)
    c_turn[np.arange(TURNS) % F, np.arange(TURNS)] = 1.0
    c_turn[np.arange(ZMAX) % RP % F, TURNS + np.arange(ZMAX)] = 1.0
    return {"c_turn": c_turn, "c_mask": mask, "c_ident": np.eye(128, dtype=np.float32), "base": np.tile(first, GS).reshape(GROWS, 1)}


def kernel(**inputs):
    import numpy as _np
    import concourse.bacc as _bacc
    from concourse import mybir as _mybir
    from concourse.bass_utils import run_bass_kernel_spmd as _run

    a = {k: _np.asarray(v) for k, v in inputs.items()}
    w0 = a["L0_rec_f0"].reshape(F, F, M)
    w0a = _np.zeros((ZMAX, ZT, M), _np.float32)
    w0b = _np.zeros((ZMAX, ZT, M), _np.float32)
    for s in range(SHIFTS):
        f = _np.arange(F)
        rows = (s % SPT) * RP + f
        w0a[rows, s // SPT] = w0[f, (f + s) % F]
        if s:
            w0b[rows, s // SPT] = w0[(f + s) % F, f]
    ids = _np.zeros((GS, F, NCH, GPC), a["ids"].dtype)
    by_chunk = a["ids"].reshape(NCH, CB, F).transpose(2, 0, 1)
    for s in range(GS):
        part = by_chunk[:, :, s * GPC:(s + 1) * GPC]
        ids[s, :, :, 0:part.shape[2]] = part
    ids[:, :, 0, :] = 0
    for s in range(GS):
        n = HEAD if s < GS - 1 else HEAD - 1
        ids[s, :, 0, 0:n] = by_chunk[:, 0, s * HEAD:s * HEAD + n]
        ids[s, :, 0, HEAD:] = by_chunk[:, 0, (s + 1) * TB:(s + 2) * TB]
    tables = [a[f"tbl_{f}"] for f in range(F)]
    arrays = {"tables": _np.concatenate(tables, axis=0)}
    arrays.update(constants(_np, [t.shape[0] for t in tables]))
    arrays.update({
        "ids": ids.reshape(GROWS, NCH * GPC),
        "w0a": w0a.reshape(ZMAX, ZT * M), "w0b": w0b.reshape(ZMAX, ZT * M),
        "w1": a["L0_rec_f1"].reshape(F, M, M).transpose(1, 0, 2).reshape(M, F * M),
        "w2": a["L0_rec_f2"].reshape(F, M, M).transpose(1, 0, 2).reshape(M, F * M),
        "W_top1": a["W_top1"], "W_top2": a["W_top2"],
        "b1": a["b_top1"].reshape(H1 // 128, 128).T, "b2": a["b_top2"].reshape(H2 // 128, 128).T,
        "w3": a["W_top3"].reshape(H2 // 128, 128).T, "dense": a["dense_ctx"].T,
    })
    nc = _bacc.Bacc("TRN2", target_bir_lowering=False, num_devices=1)
    placed, args = {}, {}
    for name, v in arrays.items():
        v = _np.ascontiguousarray(v)
        placed[f"in_{name}"] = v
        args[name] = nc.dram_tensor(f"in_{name}", v.shape, _mybir.dt.from_np(v.dtype), kind="ExternalInput").ap()
    out = nc.dram_tensor("out_y", (B, 1), _mybir.dt.float32, kind="ExternalOutput").ap()
    tower_kernel(nc, args, out)
    r = _run(nc, [placed], core_ids=[0])
    return r.results[0]["out_y"]
```
